# Optimizing a Trainium2 kernel written in Bass

```python
import numpy as np
import jax
import jax.numpy as jnp

def _softmax(x, axis=-1):
    return jax.nn.softmax(x, axis=axis)

def _gelu(x):
    return jax.nn.gelu(x, approximate=True)

def _silu(x):
    return jax.nn.silu(x)

def _sigmoid(x):
    return jax.nn.sigmoid(x)

def _layernorm(x, axis=-1, eps=1e-05):
    m = jnp.mean(x, axis=axis, keepdims=True)
    v = jnp.var(x, axis=axis, keepdims=True)
    return (x - m) / jnp.sqrt(v + eps)

def _scatter_add(tgt, idx, src, axis=0):
    return tgt.at[idx].add(src)

def _segment_sum(src, seg, n):
    return jax.ops.segment_sum(src, seg, n)
kernel_name = 'mk_xattn_ffn_d1_seqx_r8_f7d9f7'

def setup_inputs(seed: int=0):
    np.random.seed(seed)
    _w = jnp.asarray

    def _rec_inputs():
        import jax
        import jax.numpy as jnp
        _rk = jax.random.key(seed)
        x = 4.136e-05 + 0.9999 * jax.random.normal(jax.random.fold_in(_rk, 1), (4, 256, 256), jnp.float32)
        _lenS = 256 - jax.random.randint(jax.random.fold_in(_rk, 7), (4,), 0, max(1, 256 // 4) + 1, jnp.int32)
        _lenS2 = 256 - jax.random.randint(jax.random.fold_in(_rk, 8), (4,), 0, max(1, 256 // 4) + 1, jnp.int32)
        _ctx_1024P = jax.random.normal(jax.random.fold_in(_rk, 11), (4, 16, 128), jnp.float32)
        _ctx_1024c = jax.random.dirichlet(jax.random.fold_in(_rk, 511), 0.3 * jnp.ones((16,), jnp.float32), (4, 256))
        _ctx_1024t = jnp.einsum('bsk,bkd->bsd', _ctx_1024c, _ctx_1024P)
        _ctx_1024t = _ctx_1024t * jax.lax.rsqrt(jnp.mean(jnp.square(_ctx_1024t)) + 1e-12) * 0.953939
        ctx_1024 = -0.000292821 + 1.00034 * (_ctx_1024t + 0.3 * jax.random.normal(jax.random.fold_in(_rk, 611), (4, 256, 128), jnp.float32))
        return (x, ctx_1024)
    x, ctx_1024 = _rec_inputs()

    def _L0_xattn_setup():
        import jax, jax.numpy as jnp
        import numpy as np
        import math
        B, L, DM = (2, 256, 128)
        DS, DC, EXP = (16, 4, 2)
        DI = EXP * DM
        DR = math.ceil(DM / 16)
        DT_MIN, DT_MAX, DT_FLOOR = (0.001, 0.1, 0.0001)

        def _ssm_forward(hidden_states, z, in_proj_w, conv_w, conv_b, x_proj_w, dt_proj_w, dt_proj_b, A_log, D):
            b = hidden_states.shape[0]
            x = jnp.einsum('ed,bld->bel', in_proj_w, hidden_states)
            xp = jnp.pad(x, ((0, 0), (0, 0), (DC - 1, 0)))
            xc = jax.lax.conv_general_dilated(xp, conv_w[:, None, :], window_strides=(1,), padding='VALID', dimension_numbers=('NCH', 'OIH', 'NCH'), feature_group_count=DI)
            u = jax.nn.silu(xc + conv_b[None, :, None])
            x_dbl = jnp.einsum('ke,bel->bkl', x_proj_w, u)
            dt_lo = x_dbl[:, :DR]
            Bm = x_dbl[:, DR:DR + DS]
            Cm = x_dbl[:, DR + DS:]
            delta = jax.nn.softplus(jnp.einsum('er,brl->bel', dt_proj_w, dt_lo) + dt_proj_b[None, :, None])
            A = -jnp.exp(A_log)

            def step(state, xs):
                d_t, B_t, C_t, u_t = xs
                dA = jnp.exp(d_t[..., None] * A)
                state = state * dA + (d_t * u_t)[..., None] * B_t[:, None, :]
                y_t = jnp.einsum('ben,bn->be', state, C_t)
                return (state, y_t)
            xs = (jnp.moveaxis(delta, -1, 0), jnp.moveaxis(Bm, -1, 0), jnp.moveaxis(Cm, -1, 0), jnp.moveaxis(u, -1, 0))
            state0 = jnp.zeros((b, DI, DS), delta.dtype)
            _, ys = jax.lax.scan(step, state0, xs)
            y = jnp.moveaxis(ys, 0, -1)
            y = y + D[None, :, None] * u
            y = y * jax.nn.silu(z)
            return jnp.swapaxes(y, 1, 2)
        key = jax.random.key(seed)
        ks = jax.random.split(key, 8)
        hidden_states = jax.random.normal(ks[0], (B, L, DM), jnp.float32)
        z = jax.random.normal(ks[1], (B, DI, L), jnp.float32)
        in_proj_w = jax.random.normal(ks[2], (DI, DM), jnp.float32) * DM ** (-0.5)
        conv_w = jax.random.normal(ks[3], (DI, DC), jnp.float32) * DC ** (-0.5)
        conv_b = jnp.zeros((DI,), jnp.float32)
        x_proj_w = jax.random.normal(ks[4], (DR + 2 * DS, DI), jnp.float32) * DI ** (-0.5)
        dt_std = DR ** (-0.5)
        dt_proj_w = jax.random.uniform(ks[5], (DI, DR), jnp.float32, -dt_std, dt_std)
        dt = jnp.exp(jax.random.uniform(ks[6], (DI,), jnp.float32) * (math.log(DT_MAX) - math.log(DT_MIN)) + math.log(DT_MIN))
        dt = jnp.clip(dt, DT_FLOOR)
        dt_proj_b = dt + jnp.log(-jnp.expm1(-dt))
        A_log = jnp.log(jnp.broadcast_to(jnp.arange(1, DS + 1, dtype=jnp.float32), (DI, DS)))
        D = jnp.ones((DI,), jnp.float32)
        return dict(hidden_states=hidden_states, z=z, in_proj_w=in_proj_w, conv_w=conv_w, conv_b=conv_b, x_proj_w=x_proj_w, dt_proj_w=dt_proj_w, dt_proj_b=dt_proj_b, A_log=A_log, D=D)
    _L0_xattn_all = _L0_xattn_setup()
    _L0_xattn_in = {k: v for k, v in _L0_xattn_all.items() if k in ('in_proj_w', 'conv_w', 'conv_b', 'x_proj_w', 'dt_proj_w', 'dt_proj_b', 'A_log', 'D')}
    del _L0_xattn_all

    def _L0_ffn_setup():
        import jax, jax.numpy as jnp
        import numpy as np
        K = 2

        def gelu(v):
            return jax.nn.gelu(v, approximate=False)
        key = jax.random.key(seed)
        ks = jax.random.split(key, 10)
        B, S, D, H, E = (4, 256, 256, 128, 8)
        SH = 2 * H
        u = lambda k_, shape, b: jax.random.uniform(k_, shape, jnp.float32, -b, b)
        return {'x': jax.random.normal(ks[0], (B, S, D), jnp.float32), 'gate_w': u(ks[1], (D, E), 1.0 / D), 'w1': u(ks[2], (E, D, H), 1.0 / D), 'b1': u(ks[3], (E, H), 1.0 / np.sqrt(D)), 'w2': u(ks[4], (E, H, D), 1.0 / H), 'b2': u(ks[5], (E, D), 1.0 / np.sqrt(H)), 'shared_w1': u(ks[6], (D, SH), 1.0 / D), 'shared_b1': u(ks[7], (SH,), 1.0 / np.sqrt(D)), 'shared_w2': u(ks[8], (SH, D), 1.0 / SH), 'shared_b2': u(ks[9], (D,), 1.0 / np.sqrt(SH))}
    _L0_ffn_all = _L0_ffn_setup()
    _L0_ffn_in = {k: v for k, v in _L0_ffn_all.items() if k in ('gate_w', 'w1', 'b1', 'w2', 'b2', 'shared_w1', 'shared_b1', 'shared_w2', 'shared_b2')}
    del _L0_ffn_all
    return {'x': x, 'ctx_1024': ctx_1024, 'L0_xattn_in_proj_w': _L0_xattn_in['in_proj_w'], 'L0_xattn_conv_w': _L0_xattn_in['conv_w'], 'L0_xattn_conv_b': _L0_xattn_in['conv_b'], 'L0_xattn_x_proj_w': _L0_xattn_in['x_proj_w'], 'L0_xattn_dt_proj_w': _L0_xattn_in['dt_proj_w'], 'L0_xattn_dt_proj_b': _L0_xattn_in['dt_proj_b'], 'L0_xattn_A_log': _L0_xattn_in['A_log'], 'L0_xattn_D': _L0_xattn_in['D'], 'L0_ffn_gate_w': _L0_ffn_in['gate_w'], 'L0_ffn_w1': _L0_ffn_in['w1'], 'L0_ffn_b1': _L0_ffn_in['b1'], 'L0_ffn_w2': _L0_ffn_in['w2'], 'L0_ffn_b2': _L0_ffn_in['b2'], 'L0_ffn_shared_w1': _L0_ffn_in['shared_w1'], 'L0_ffn_shared_b1': _L0_ffn_in['shared_b1'], 'L0_ffn_shared_w2': _L0_ffn_in['shared_w2'], 'L0_ffn_shared_b2': _L0_ffn_in['shared_b2']}

def reference(x, ctx_1024, L0_xattn_in_proj_w, L0_xattn_conv_w, L0_xattn_conv_b, L0_xattn_x_proj_w, L0_xattn_dt_proj_w, L0_xattn_dt_proj_b, L0_xattn_A_log, L0_xattn_D, L0_ffn_gate_w, L0_ffn_w1, L0_ffn_b1, L0_ffn_w2, L0_ffn_b2, L0_ffn_shared_w1, L0_ffn_shared_b1, L0_ffn_shared_w2, L0_ffn_shared_b2):
    import jax
    import jax.numpy as jnp

    def _L0_xattn_ref(hidden_states, z, in_proj_w, conv_w, conv_b, x_proj_w, dt_proj_w, dt_proj_b, A_log, D):
        import jax, jax.numpy as jnp
        import numpy as np
        import math
        B, L, DM = (2, 256, 128)
        DS, DC, EXP = (16, 4, 2)
        DI = EXP * DM
        DR = math.ceil(DM / 16)
        DT_MIN, DT_MAX, DT_FLOOR = (0.001, 0.1, 0.0001)

        def _ssm_forward(hidden_states, z, in_proj_w, conv_w, conv_b, x_proj_w, dt_proj_w, dt_proj_b, A_log, D):
            b = hidden_states.shape[0]
            x = jnp.einsum('ed,bld->bel', in_proj_w, hidden_states)
            xp = jnp.pad(x, ((0, 0), (0, 0), (DC - 1, 0)))
            xc = jax.lax.conv_general_dilated(xp, conv_w[:, None, :], window_strides=(1,), padding='VALID', dimension_numbers=('NCH', 'OIH', 'NCH'), feature_group_count=DI)
            u = jax.nn.silu(xc + conv_b[None, :, None])
            x_dbl = jnp.einsum('ke,bel->bkl', x_proj_w, u)
            dt_lo = x_dbl[:, :DR]
            Bm = x_dbl[:, DR:DR + DS]
            Cm = x_dbl[:, DR + DS:]
            delta = jax.nn.softplus(jnp.einsum('er,brl->bel', dt_proj_w, dt_lo) + dt_proj_b[None, :, None])
            A = -jnp.exp(A_log)

            def step(state, xs):
                d_t, B_t, C_t, u_t = xs
                dA = jnp.exp(d_t[..., None] * A)
                state = state * dA + (d_t * u_t)[..., None] * B_t[:, None, :]
                y_t = jnp.einsum('ben,bn->be', state, C_t)
                return (state, y_t)
            xs = (jnp.moveaxis(delta, -1, 0), jnp.moveaxis(Bm, -1, 0), jnp.moveaxis(Cm, -1, 0), jnp.moveaxis(u, -1, 0))
            state0 = jnp.zeros((b, DI, DS), delta.dtype)
            _, ys = jax.lax.scan(step, state0, xs)
            y = jnp.moveaxis(ys, 0, -1)
            y = y + D[None, :, None] * u
            y = y * jax.nn.silu(z)
            return jnp.swapaxes(y, 1, 2)
        return _ssm_forward(hidden_states, z, in_proj_w, conv_w, conv_b, x_proj_w, dt_proj_w, dt_proj_b, A_log, D)

    def _L0_ffn_ref(x, gate_w, w1, b1, w2, b2, shared_w1, shared_b1, shared_w2, shared_b2):
        import jax, jax.numpy as jnp
        import numpy as np
        K = 2

        def gelu(v):
            return jax.nn.gelu(v, approximate=False)
        B, S, D = x.shape
        E = gate_w.shape[1]
        xf = x.reshape(-1, D)
        logits = xf @ gate_w
        top_logits, top_idx = jax.lax.top_k(logits, K)
        top_gates = jax.nn.softmax(top_logits, axis=-1)
        gates = jnp.sum(jax.nn.one_hot(top_idx, E, dtype=xf.dtype) * top_gates[..., None], axis=1)
        h = gelu(jnp.einsum('nd,edh->neh', xf, w1) + b1)
        out_e = jnp.einsum('neh,ehd->ned', h, w2) + b2
        routed = jnp.einsum('ne,ned->nd', gates, out_e)
        shared = gelu(xf @ shared_w1 + shared_b1) @ shared_w2 + shared_b2
        return (routed + shared).reshape(B, S, D)
    x = x + _L0_xattn_ref(ctx_1024, _layernorm(x, axis=-1), L0_xattn_in_proj_w, L0_xattn_conv_w, L0_xattn_conv_b, L0_xattn_x_proj_w, L0_xattn_dt_proj_w, L0_xattn_dt_proj_b, L0_xattn_A_log, L0_xattn_D)
    x = x + _L0_ffn_ref(_layernorm(x, axis=-1), L0_ffn_gate_w, L0_ffn_w1, L0_ffn_b1, L0_ffn_w2, L0_ffn_b2, L0_ffn_shared_w1, L0_ffn_shared_b1, L0_ffn_shared_w2, L0_ffn_shared_b2)
    return x

_drawn_inputs = setup_inputs


def setup_inputs(seed=0):
    import zlib

    import numpy as np

    out = dict(_drawn_inputs(seed))
    spreads = {'L0_xattn_conv_b': (0.0, 0.1), 'L0_xattn_D': (1.0, 0.2)}
    factors = {'L0_xattn_dt_proj_w': 5.953,
     'L0_ffn_w1': 8.0,
     'L0_ffn_b1': 8.0,
     'L0_ffn_w2': 8.0,
     'L0_ffn_shared_w1': 8.0,
     'L0_ffn_shared_b1': 8.0,
     'L0_ffn_shared_w2': 8.0}
    for name, (base, spread) in spreads.items():
        noise = np.random.default_rng([zlib.crc32(name.encode()), seed]).standard_normal(out[name].shape)
        drawn = base * np.exp(spread * noise) if base else spread * noise
        out[name] = jnp.asarray(drawn.astype(out[name].dtype))
    for name, factor in factors.items():
        out[name] = (out[name] * factor).astype(out[name].dtype)
    return out
```

```python
from contextlib import ExitStack

import concourse.bass as bass
from concourse import mybir

F32 = mybir.dt.float32
BF16 = mybir.dt.bfloat16
U32 = mybir.dt.uint32
ALU = mybir.AluOpType
ACT = mybir.ActivationFunctionType

P = 128
LN_EPS = 1e-5


def mamba_xattn_moe_ffn(
    nc: bass.Bass,
    x_in: bass.AP,
    ctx_in: bass.AP,
    in_proj_w: bass.AP,
    conv_w: bass.AP,
    conv_b: bass.AP,
    x_proj_w: bass.AP,
    dt_proj_w: bass.AP,
    dt_proj_b: bass.AP,
    A_log: bass.AP,
    D_skip: bass.AP,
    gate_w: bass.AP,
    w1: bass.AP,
    b1: bass.AP,
    w2: bass.AP,
    b2: bass.AP,
    shared_w1: bass.AP,
    shared_b1: bass.AP,
    shared_w2: bass.AP,
    shared_b2: bass.AP,
    out: bass.AP,
):
    B, L, DI = x_in.shape
    DM = ctx_in.shape[2]
    DC = conv_w.shape[1]
    DR = dt_proj_w.shape[1]
    DS = A_log.shape[1]
    NE, D, H = w1.shape
    CH = DI // P
    LT = L // P
    T = B * LT
    PAIRS = B // 2
    BP = B // PAIRS
    W = BP * L
    TP = T // PAIRS
    UNITS = DS * CH
    SH = shared_w1.shape[1]
    HC = NE + SH // P
    PAD = DC - 1
    LP = L + PAD + 1
    assert DM == P and D == DI and H == P and W == 512 and CH == 2 and LT == 2
    BC = 2 * DS
    assert BC == 32
    XR = 3 * BC + DR

    with ExitStack() as ctx:

        def sb(name, shape, dt=F32):
            return ctx.enter_context(nc.sbuf_tensor(name, shape, dt))

        def sem(name):
            return ctx.enter_context(nc.semaphore(name))

        x = sb("x", [P, T, D])
        ctx_nat = sb("ctx_nat", [P, T, DM])
        ctxT = sb("ctxT", [P, B, LP])
        w_in = sb("w_in", [P, CH, DM])
        cw = sb("cw", [P, CH, DC])
        rows = sb("rows", [3 * CH + HC, P])
        cols = sb("cols", [P, 3 * CH + HC])
        cb = cols[:, 0:CH]
        dtb = cols[:, CH:2 * CH]
        dsk = cols[:, 2 * CH:3 * CH]
        b1T = cols[:, 3 * CH:3 * CH + HC]
        alog = sb("alog", [P, CH, DS])
        aneg = sb("aneg", [P, CH, DS])
        w_taps = sb("w_taps", [P, CH, DC, DM])
        w_tapsT = sb("w_tapsT", [P, CH, DC, P])
        xp_nat = sb("xp_nat", [XR, DI])
        xpT = sb("xpT", [P, CH, XR])
        dt_nat = sb("dt_nat", [P, CH, P])
        dtT = sb("dtT", [P, CH, P])
        ident = sb("ident", [P, P])
        selector = sb("selector", [3 * BC, BC, P], BF16)
        u = sb("u", [P, PAIRS, CH, W])
        sz = sb("sz", [P, PAIRS, CH, W])
        minus_half = sb("minus_half", [P, T])
        zstat = sb("zstat", [P, T, 6])
        zmv = sb("zmv", [P, T, 2])
        zrstd = sb("zrstd", [P, T])
        znmr = sb("znmr", [P, T])
        xdt = sb("xdt", [P, W])
        xc = sb("xc", [P, CH, W])
        bc3 = sb("bc3", [3 * BC, PAIRS, W], BF16)
        bc_rest = sb("bc_rest", [3 * BC, W])
        bc_mid = sb("bc_mid", [3 * BC, W], BF16)
        vb = sb("vb", [P, CH, W])
        sp = sb("sp", [P, CH, W])
        delta = sb("delta", [P, PAIRS, CH, W])
        du = sb("du", [P, PAIRS, CH, W])
        c_bc = sb("c_bc", [P, 2, W])
        dbu = sb("dbu", [P, 3, W])
        hst = sb("hst", [P, 3, W])
        hc = sb("hc", [P, 3, W])
        yt = sb("yt", [P, CH, W])
        yf = sb("yf", [P, CH, W])
        nstat = sb("nstat", [P, T, 6])
        nmv = sb("nmv", [P, T, 2])
        nrstd = sb("nrstd", [P, T])
        xf = sb("xf", [P, T, D])
        xfT = sb("xfT", [P, CH, T * P])
        gw = sb("gw", [P, CH, NE])
        lg = sb("lg", [P, T, NE])
        mx = sb("mx", [P, T, 8])
        mi = sb("mi", [P, T, 8], U32)
        mif = sb("mif", [P, T, 2])
        gd = sb("gd", [P, T])
        ge = sb("ge", [P, T])
        gs = sb("gs", [P, T])
        g12 = sb("g12", [P, T, 2])
        experts = sb("experts", [P, NE])
        hot = sb("hot", [P, T, 2, NE])
        gates = sb("gates", [P, T, NE + 1])
        gatesT = sb("gatesT", [NE + 1, T * P])
        b2a = sb("b2a", [NE + 1, D])
        w_up = sb("w_up", [P, CH, HC, H])
        w_dn = sb("w_dn", [P, HC, D])
        hid = sb("hid", [P, 3, W])

        bank = [ctx.enter_context(nc.psum_tensor(f"bank{i}", [P, 512], F32)) for i in range(8)]
        p_b = [bank[0], bank[1]]
        p_c = bank[2]
        p_a = [bank[3], bank[4]]
        p_y = [bank[5], bank[6]]
        p_m = bank[7]
        p_o = [p_c, p_a[0], p_a[1]]

        l_ctx = [sem(f"l_ctx{q}") for q in range(PAIRS)]
        l_win = sem("l_win")
        l_xp = sem("l_xp")
        l_dt = sem("l_dt")
        l_vec = sem("l_vec")
        l_alog = sem("l_alog")
        l_x = sem("l_x")
        l_gw = sem("l_gw")
        l_b2 = sem("l_b2")
        l_up = sem("l_up")
        l_dn = sem("l_dn")
        k_ident = sem("k_ident")
        k_sel = sem("k_sel")
        k_pool = sem("k_pool")
        k_const = sem("k_const")
        k_zero = sem("k_zero")
        s_taps = sem("s_taps")
        t_taps = sem("t_taps")
        e_taps = sem("e_taps")
        t_ctx = sem("t_ctx")
        e_ctx = sem("e_ctx")
        t_xp = sem("t_xp")
        e_xp = sem("e_xp")
        t_dt = sem("t_dt")
        e_dt = sem("e_dt")
        e_cols = sem("e_cols")
        s_xcb = sem("s_xcb")
        s_aneg = sem("s_aneg")
        s_xc = sem("s_xc")
        s_u = sem("s_u")
        s_zst = sem("s_zst")
        s_zmv = sem("s_zmv")
        s_zr = sem("s_zr")
        s_z = sem("s_z")
        s_sz = sem("s_sz")
        s_xd = sem("s_xd")
        s_xdt = sem("s_xdt")
        s_hi = sem("s_hi")
        s_rest = sem("s_rest")
        s_mid = sem("s_mid")
        s_bc3 = sem("s_bc3")
        s_v = sem("s_v")
        s_vb = sem("s_vb")
        s_sp = sem("s_sp")
        s_delta = sem("s_delta")
        s_du = sem("s_du")
        s_B = sem("s_B")
        s_C = sem("s_C")
        s_cbc = sem("s_cbc")
        s_decay = sem("s_decay")
        s_dbu = sem("s_dbu")
        s_h = sem("s_h")
        s_hc = sem("s_hc")
        s_y = sem("s_y")
        s_yt = sem("s_yt")
        s_yf = sem("s_yf")
        s_yT = sem("s_yT")
        s_x2 = sem("s_x2")
        s_nst = sem("s_nst")
        s_nmv = sem("s_nmv")
        s_nr = sem("s_nr")
        s_xf = sem("s_xf")
        s_xfT = sem("s_xfT")
        s_xfTe = sem("s_xfTe")
        s_lg = sem("s_lg")
        s_lge = sem("s_lge")
        s_mx = sem("s_mx")
        s_mi = sem("s_mi")
        s_gd = sem("s_gd")
        s_ge = sem("s_ge")
        s_g = sem("s_g")
        s_gates = sem("s_gates")
        s_gT = sem("s_gT")
        s_gTe = sem("s_gTe")
        s_up = sem("s_up")
        s_hid = sem("s_hid")
        s_dn = sem("s_dn")
        s_acc = sem("s_acc")
        s_out = sem("s_out")

        x_tok = x_in.rearrange("b (t p) d -> p (b t) d", p=P)
        out_tok = out.rearrange("b (t p) d -> p (b t) d", p=P)
        ctx_tok = ctx_in.rearrange("b (t p) d -> p (b t) d", p=P)

        def as_rows(v):
            return v.rearrange("(c p) -> c p", p=P)

        def chans(v):
            return v.rearrange("(c p) k -> p c k", p=P)

        def batches(ap):
            return ap.rearrange("p (b l) -> p b l", b=BP)

        def conv_out(q, c):
            return p_y[c] if q == 0 else p_m

        def dt_out(q, c):
            return p_b[c] if q == 0 else p_m

        def groups_with(m):
            q, j = divmod(m, HC)
            return q * (NE + 1) + min(j, NE) + 1

        block = ctx.enter_context(nc.Block())

        @block.sync
        def _(sp_):
            for q in range(PAIRS):
                sp_.dma_start(ctx_nat[:, q * TP:(q + 1) * TP, :], ctx_tok[:, q * TP:(q + 1) * TP, :]).then_inc(l_ctx[q], 16)
            for r in range(3):
                sp_.dma_start(xp_nat[r * BC:(r + 1) * BC, :], x_proj_w[DR:DR + BC, :]).then_inc(l_xp, 16)
            sp_.dma_start(xp_nat[3 * BC:XR, :], x_proj_w[0:DR, :]).then_inc(l_xp, 16)
            sp_.dma_start(x[:, :, :], x_tok).then_inc(l_x, 16)
            for c in range(CH):
                sp_.dma_start(w_up[:, c, 0:NE, :], w1[:, c * P:(c + 1) * P, :].rearrange("e p h -> p e h")).then_inc(l_up, 16)
                sp_.dma_start(w_up[:, c, NE:HC, :], shared_w1[c * P:(c + 1) * P, :].rearrange("p (j h) -> p j h", h=H)).then_inc(l_up, 16)
            sp_.dma_start(w_dn[:, 0:NE, :], w2.rearrange("e p d -> p e d")).then_inc(l_dn, 16)
            sp_.dma_start(w_dn[:, NE:HC, :], shared_w2.rearrange("(j p) d -> p j d", p=P)).then_inc(l_dn, 16)
            for q in range(PAIRS):
                for t in range(TP):
                    sp_.wait_ge(s_acc, q * TP * (NE + 1) + TP * NE + t + 1)
                    sp_.dma_start(out_tok[:, q * TP + t, :], x[:, q * TP + t, :]).then_inc(s_out, 16)
            sp_.wait_ge(s_out, 16 * T)

        @block.gpsimd
        def _(pool):
            nc.gpsimd.memset(ident[:], 0.0).then_inc(k_pool, 1)
            pool.wait_ge(k_pool, 1)
            nc.gpsimd.affine_select(out=ident[:], in_=ident[:], compare_op=ALU.not_equal, fill=1.0, base=0,
                                    pattern=[[-1, P]], channel_multiplier=1).then_inc(k_ident, 1)
            nc.gpsimd.memset(ctxT[:, :, 0:PAD], 0.0).then_inc(k_const, 1)
            nc.gpsimd.memset(selector[:], 0.0).then_inc(k_pool, 1)
            pool.wait_ge(k_pool, 2)
            for r in range(3):
                nc.gpsimd.affine_select(out=selector[:], in_=selector[:], compare_op=ALU.not_equal, fill=1.0,
                                        base=-BC * r, pattern=[[-1, BC], [0, P]], channel_multiplier=1).then_inc(k_sel, 1)
                pool.wait_ge(k_sel, r + 1)
            nc.gpsimd.memset(minus_half[:], -0.5).then_inc(k_const, 1)
            pool.wait_ge(k_const, 2)
            nc.gpsimd.iota(experts[:], [[1, NE]], base=0, channel_multiplier=0,
                           allow_small_or_imprecise_dtypes=True).then_inc(k_const, 1)
            nc.gpsimd.memset(gates[:, :, NE:NE + 1], 1.0).then_inc(k_const, 1)

            def rstd(o, var, steps, done):
                nc.gpsimd.tensor_scalar(o, var, LN_EPS, None, ALU.add).then_inc(k_pool, 1)
                pool.wait_ge(k_pool, steps)
                nc.gpsimd.tensor_tensor(o, o, minus_half[:, 0:var.shape[1]], ALU.pow).then_inc(done, 1)

            pool.wait_ge(s_zmv, T)
            rstd(zrstd[:], zmv[:, :, 1], 3, s_zr)

            def token_rstd(q):
                a, b = q * TP, (q + 1) * TP
                pool.wait_ge(s_nmv, b)
                rstd(nrstd[:, a:b], nmv[:, a:b, 1], 4 + q, s_nr)

            for q in range(PAIRS):
                for n in range(DS):
                    if q == 1 and n == 5:
                        token_rstd(0)
                    for c in range(CH):
                        i = (q * DS + n) * CH + c
                        pool.wait_ge(s_h, i + 1)
                        pool.wait_ge(s_cbc, q * DS + n + 1)
                        if i >= 3:
                            pool.wait_ge(s_y, i - 2)
                        nc.gpsimd.tensor_tensor(hc[:, i % 3, :], hst[:, i % 3, :], c_bc[:, n % 2, :], ALU.mult).then_inc(s_hc, 1)
            token_rstd(1)

        @block.scalar
        def _(act):
            act.dma_start(w_in[:], chans(in_proj_w)).then_inc(l_win, 16)
            act.dma_start(cw[:], chans(conv_w)).then_inc(l_win, 16)
            for r, v in enumerate((conv_b, dt_proj_b, D_skip, shared_b1)):
                at = r * CH if r < 3 else 3 * CH + NE
                act.dma_start(rows[at:at + CH, :], as_rows(v)).then_inc(l_vec, 16)
            act.dma_start(rows[3 * CH:3 * CH + NE, :], b1).then_inc(l_vec, 16)
            act.dma_start(alog[:], chans(A_log)).then_inc(l_alog, 16)
            act.wait_ge(k_zero, 1)
            act.dma_start(dt_nat[:, :, 3 * BC:XR], chans(dt_proj_w)).then_inc(l_dt, 16)
            act.dma_start(b2a[0:NE, :], b2).then_inc(l_b2, 16)
            act.dma_start(b2a[NE:NE + 1, :], shared_b2.rearrange("(a d) -> a d", a=1)).then_inc(l_b2, 16)
            act.dma_start(gw[:], chans(gate_w)).then_inc(l_gw, 16)

            act.wait_ge(t_taps, 2)
            nc.scalar.copy(w_tapsT[:, 1], p_y[1][:]).then_inc(e_taps, 1)

            def silus(q):
                for c in range(CH):
                    if q == 0:
                        act.wait_ge(s_xc, c + 1)
                        act.wait_ge(e_cols, 1)
                        nc.scalar.activation(u[:, q, c, :], conv_out(q, c)[:], ACT.Silu, bias=cb[:, c:c + 1]).then_inc(s_u, 1)
                    else:
                        act.wait_ge(s_xcb, c + 1)
                        nc.scalar.activation(u[:, q, c, :], xc[:, c, :], ACT.Silu).then_inc(s_u, 1)
                if q == 0:
                    act.wait_ge(s_z, 1)
                for t in range(q * TP, (q + 1) * TP):
                    b, c = divmod(t - q * TP, LT)
                    nc.scalar.activation(sz[:, q, c, b * L:(b + 1) * L], x[:, t, :], ACT.Silu, scale=zrstd[:, t:t + 1],
                                         bias=znmr[:, t:t + 1]).then_inc(s_sz, 1)

            def keep_conv(c):
                act.wait_ge(s_xc, CH + c + 1)
                nc.scalar.activation(xc[:, c, :], conv_out(1, c)[:], ACT.Identity, bias=cb[:, c:c + 1]).then_inc(s_xcb, 1)

            def dt_rows(q):
                act.wait_ge(s_xd, q + 1)
                if q:
                    act.wait_ge(s_v, q * CH)
                nc.scalar.copy(xdt[3 * BC:XR, :], p_m[3 * BC:XR, :]).then_inc(s_xdt, 1)

            def softplus_log(q):
                act.wait_ge(s_vb, (q + 1) * CH)
                if q:
                    act.wait_ge(s_delta, q)
                nc.scalar.activation(sp[:], vb[:], ACT.Abs).then_inc(s_sp, 1)
                act.wait_ge(s_sp, 3 * q + 1)
                nc.scalar.activation(sp[:], sp[:], ACT.Exp, scale=-1.0).then_inc(s_sp, 1)
                act.wait_ge(s_sp, 3 * q + 2)
                nc.scalar.activation(sp[:], sp[:], ACT.Ln, bias=1.0).then_inc(s_sp, 1)

            def gate_exp(q):
                act.wait_ge(s_gd, q + 1)
                nc.scalar.activation(ge[:, q * TP:(q + 1) * TP], gd[:, q * TP:(q + 1) * TP], ACT.Exp).then_inc(s_ge, 1)

            def spread_C(q, n):
                k = q * DS + n
                act.wait_ge(s_C, k + 1)
                if k >= 2:
                    act.wait_ge(s_hc, (k - 1) * CH)
                nc.scalar.copy(c_bc[:, n % 2, :], p_c[:]).then_inc(s_cbc, 1)

            def xfT_out(q, c):
                act.wait_ge(s_xfT, q * CH + c + 1)
                nc.scalar.copy(xfT[:, c, q * W:(q + 1) * W], p_m[:]).then_inc(s_xfTe, 1)

            silus(0)
            nc.scalar.preload_act_table_set("natural_log_exp_and_others")
            act.wait_ge(l_alog, 16)
            nc.scalar.activation(aneg[:], alog[:], ACT.Exp).then_inc(s_aneg, 1)
            dt_rows(0)
            softplus_log(0)
            act.wait_ge(s_aneg, 2)
            act.wait_ge(k_zero, 3)
            for q in range(PAIRS):
                act.wait_ge(s_delta, q + 1)
                for n in range(DS):
                    spread_C(q, n)
                    for c in range(CH):
                        i = (q * DS + n) * CH + c
                        if i >= 2:
                            act.wait_ge(s_h, i - 1)
                        nc.scalar.activation(batches(p_a[i % 2][:])[:, :, 1:L], batches(delta[:, q, c, :])[:, :, 1:L],
                                             ACT.Exp, scale=aneg[:, c, n:n + 1]).then_inc(s_decay, 1)
                    if q == 0 and n in (2, 4):
                        keep_conv(n // 2 - 1)
                    if q == 0 and n == 5:
                        silus(1)
                        nc.scalar.preload_act_table_set("natural_log_exp_and_others")
                    if q == 0 and n == 7:
                        dt_rows(1)
                    if q == 0 and n == 11:
                        softplus_log(1)
                    if q == 1 and n in (9, 10):
                        xfT_out(0, n - 9)
                    if q == 1 and n == 13:
                        gate_exp(0)
            for q in range(PAIRS):
                for j in range(HC):
                    m = q * HC + j
                    act.wait_ge(s_up, m + 1)
                    if m >= 3:
                        act.wait_ge(s_dn, 2 * groups_with(m - 3))
                    nc.scalar.activation(hid[:, m % 3, :], p_b[m % 2][:], ACT.Gelu, bias=b1T[:, j:j + 1]).then_inc(s_hid, 1)
                    if q == 0 and j in (5, 6):
                        xfT_out(1, j - 5)
                    if q == 0 and j == 8:
                        gate_exp(1)

        @block.vector
        def _(dve):
            nc.vector.memset(dt_nat[:], 0.0).then_inc(k_zero, 1)
            for a in p_a:
                nc.vector.memset(batches(a[:])[:, :, 0:1], 0.0).then_inc(k_zero, 1)
            dve.wait_ge(l_win, 32)
            for c in range(CH):
                for k in range(DC):
                    nc.vector.tensor_scalar(w_taps[:, c, k, :], w_in[:, c, :], cw[:, c, k:k + 1], None, ALU.mult).then_inc(s_taps, 1)
            dve.wait_ge(k_const, 1)
            for q in range(PAIRS):
                dve.wait_ge(t_ctx, q + 1)
                nc.vector.tensor_copy(ctxT[:, q * BP:(q + 1) * BP, PAD:PAD + L], batches(p_b[q][:])).then_inc(e_ctx, 1)
                if q == 0:
                    dve.wait_ge(t_taps, 1)
                    nc.vector.tensor_copy(w_tapsT[:, 0], p_y[0][:].rearrange("p (k d) -> p k d", k=DC)).then_inc(e_taps, 1)
            dve.wait_ge(t_xp, 1)
            nc.vector.tensor_copy(xpT[:], p_c[:, 0:CH * XR].rearrange("p (c r) -> p c r", c=CH)).then_inc(e_xp, 1)
            dve.wait_ge(t_dt, 1)
            nc.vector.tensor_copy(dtT[:], p_m[:, 0:CH * P].rearrange("p (c e) -> p c e", c=CH)).then_inc(e_dt, 1)

            nc.vector.tensor_copy(cols[:], p_m[:, CH * P:CH * P + 3 * CH + HC]).then_inc(e_cols, 1)

            dve.wait_ge(l_x, 16)
            for t in range(T):
                nc.vector.bn_stats(zstat[:, t, :], x[:, t, :]).then_inc(s_zst, 1)
            for t in range(T):
                dve.wait_ge(s_zst, t + 1)
                nc.vector.bn_aggr(zmv[:, t, :], zstat[:, t, :]).then_inc(s_zmv, 1)
            dve.wait_ge(s_zr, 1)
            nc.vector.scalar_tensor_tensor(znmr[:], zmv[:, :, 0], -1.0, zrstd[:], ALU.mult, ALU.mult).then_inc(s_z, 1)

            def split_bc(q):
                dve.wait_ge(s_xd, q + 1)
                bcq = bc3[:, q, :]
                nc.vector.tensor_copy(bcq, p_m[0:3 * BC, :]).then_inc(s_hi, 1)
                dve.wait_ge(s_hi, q + 1)
                if q:
                    dve.wait_ge(s_bc3, 2 * q)
                nc.vector.tensor_tensor(bc_rest[:], p_m[0:3 * BC, :], bcq, ALU.subtract).then_inc(s_rest, 1)
                dve.wait_ge(s_rest, q + 1)
                nc.vector.tensor_copy(bc_mid[2 * BC:3 * BC, :], bc_rest[2 * BC:3 * BC, :]).then_inc(s_mid, 1)
                nc.vector.tensor_copy(bc3[BC:2 * BC, q, :], bc_rest[BC:2 * BC, :]).then_inc(s_bc3, 1)
                dve.wait_ge(s_mid, q + 1)
                nc.vector.tensor_tensor(bc3[2 * BC:3 * BC, q, :], bc_rest[2 * BC:3 * BC, :], bc_mid[2 * BC:3 * BC, :],
                                        ALU.subtract).then_inc(s_bc3, 1)

            def dt_bias(q, c):
                dve.wait_ge(s_v, q * CH + c + 1)
                nc.vector.tensor_scalar(vb[:, c, :], dt_out(q, c)[:], dtb[:, c:c + 1], None, ALU.add).then_inc(s_vb, 1)

            def softplus_end(q):
                dve.wait_ge(s_sp, 3 * (q + 1))
                nc.vector.scalar_tensor_tensor(delta[:, q], vb[:], 0.0, sp[:], ALU.max, ALU.add).then_inc(s_delta, 1)
                dve.wait_ge(s_delta, q + 1)
                nc.vector.tensor_tensor(du[:, q], delta[:, q], u[:, q], ALU.mult).then_inc(s_du, 1)

            def drive(i):
                q, n, c = i // UNITS, i % UNITS // CH, i % CH
                if i % UNITS == 0:
                    dve.wait_ge(s_du, q + 1)
                dve.wait_ge(s_B, q * DS + n + 1)
                if i >= 3:
                    dve.wait_ge(s_h, i - 2)
                nc.vector.tensor_tensor(dbu[:, i % 3, :], du[:, q, c, :], p_b[n % 2][:], ALU.mult).then_inc(s_dbu, 1)

            def scan(i):
                dve.wait_ge(s_dbu, i + 1)
                dve.wait_ge(s_decay, i + 1)
                if i >= 3:
                    dve.wait_ge(s_hc, i - 2)
                nc.vector.tensor_tensor_scan(hst[:, i % 3, :], p_a[i % 2][:], dbu[:, i % 3, :], 0.0, ALU.mult,
                                             ALU.add).then_inc(s_h, 1)

            def finish_y(q):
                dve.wait_ge(s_y, (q + 1) * UNITS)
                dve.wait_ge(s_sz, (q + 1) * TP)
                if q:
                    dve.wait_ge(s_yT, q * TP)
                for c in range(CH):
                    nc.vector.scalar_tensor_tensor(yt[:, c, :], u[:, q, c, :], dsk[:, c:c + 1], p_y[c][:], ALU.mult,
                                                   ALU.add).then_inc(s_yt, 1)
                for c in range(CH):
                    dve.wait_ge(s_yt, q * CH + c + 1)
                    nc.vector.tensor_tensor(yf[:, c, :], yt[:, c, :], sz[:, q, c, :], ALU.mult).then_inc(s_yf, 1)

            def residual(q, g):
                t = q * TP + 2 * g
                dve.wait_ge(s_yT, t + 2)
                nc.vector.tensor_tensor(x[:, t:t + 2, :], x[:, t:t + 2, :], p_m[:].rearrange("p (t d) -> p t d", t=2),
                                        ALU.add).then_inc(s_x2, 1)

            def norm(q):
                a, b = q * TP, (q + 1) * TP
                dve.wait_ge(s_x2, b // 2)
                for t in range(a, b):
                    nc.vector.bn_stats(nstat[:, t, :], x[:, t, :]).then_inc(s_nst, 1)
                for t in range(a, b):
                    dve.wait_ge(s_nst, t + 1)
                    nc.vector.bn_aggr(nmv[:, t, :], nstat[:, t, :]).then_inc(s_nmv, 1)

            def norm_scale(q):
                a, b = q * TP, (q + 1) * TP
                dve.wait_ge(s_nr, q + 1)
                for t in range(a, b):
                    nc.vector.tensor_scalar(xf[:, t, :], x[:, t, :], nmv[:, t, 0:1], nrstd[:, t:t + 1], ALU.subtract,
                                            ALU.mult).then_inc(s_xf, 1)

            def top2(q):
                a, b = q * TP, (q + 1) * TP
                dve.wait_ge(s_lg, q + 1)
                nc.vector.tensor_copy(lg[:, a:b, :], p_m[:, 0:TP * NE].rearrange("p (t e) -> p t e", t=TP)).then_inc(s_lge, 1)
                dve.wait_ge(s_lge, q + 1)
                for t in range(a, b):
                    nc.vector.max(mx[:, t, :], lg[:, t, :]).then_inc(s_mx, 1)
                for t in range(a, b):
                    dve.wait_ge(s_mx, t + 1)
                    nc.vector.max_index(mi[:, t, :], mx[:, t, :], lg[:, t, :]).then_inc(s_mi, 1)
                nc.vector.tensor_tensor(gd[:, a:b], mx[:, a:b, 1], mx[:, a:b, 0], ALU.subtract).then_inc(s_gd, 1)
                dve.wait_ge(s_mi, b)
                nc.vector.tensor_copy(mif[:, a:b, :], mi[:, a:b, 0:2]).then_inc(s_g, 1)

            def gate(q):
                a, b = q * TP, (q + 1) * TP
                g = 8 * q
                dve.wait_ge(s_ge, q + 1)
                nc.vector.tensor_scalar(gs[:, a:b], ge[:, a:b], 1.0, None, ALU.add).then_inc(s_g, 1)
                dve.wait_ge(s_g, g + 2)
                nc.vector.reciprocal(g12[:, a:b, 0], gs[:, a:b]).then_inc(s_g, 1)
                dve.wait_ge(s_g, g + 3)
                nc.vector.tensor_tensor(g12[:, a:b, 1], ge[:, a:b], g12[:, a:b, 0], ALU.mult).then_inc(s_g, 1)
                dve.wait_ge(k_const, 4)
                for r in range(2):
                    nc.vector.tensor_tensor(hot[:, a:b, r, :], experts[:].unsqueeze(1).to_broadcast([P, TP, NE]),
                                            mif[:, a:b, r:r + 1].to_broadcast([P, TP, NE]), ALU.is_equal).then_inc(s_g, 1)
                    dve.wait_ge(s_g, g + 5 + r)
                for r in range(2):
                    nc.vector.tensor_tensor(hot[:, a:b, r, :], hot[:, a:b, r, :],
                                            g12[:, a:b, r:r + 1].to_broadcast([P, TP, NE]), ALU.mult).then_inc(s_g, 1)
                dve.wait_ge(s_g, g + 8)
                nc.vector.tensor_tensor(gates[:, a:b, 0:NE], hot[:, a:b, 0, :], hot[:, a:b, 1, :], ALU.add).then_inc(s_gates, 1)

            def gatesT_out(q):
                dve.wait_ge(s_gT, q + 1)
                nc.vector.tensor_copy(gatesT[:, q * W:(q + 1) * W], p_m[0:NE + 1, :]).then_inc(s_gTe, 1)

            dve.wait_ge(s_aneg, 1)
            nc.vector.tensor_scalar(aneg[:], aneg[:], -1.0, None, ALU.mult).then_inc(s_aneg, 1)
            split_bc(0)
            for c in range(CH):
                dt_bias(0, c)
            softplus_end(0)
            drive(0)
            for q in range(PAIRS):
                for n in range(DS):
                    for c in range(CH):
                        i = (q * DS + n) * CH + c
                        if i + 1 < PAIRS * UNITS:
                            drive(i + 1)
                        scan(i)
                    if q == 0:
                        if n == 7:
                            split_bc(1)
                        if n == 9:
                            dt_bias(1, 0)
                        if n == 10:
                            dt_bias(1, 1)
                        if n == 13:
                            softplus_end(1)
                    if q == 1:
                        if n == 0:
                            finish_y(0)
                        if n == 2:
                            residual(0, 0)
                        if n == 4:
                            residual(0, 1)
                            norm(0)
                        if n == 6:
                            norm_scale(0)
                        if n == 12:
                            top2(0)
                        if n == 14:
                            gate(0)
            gatesT_out(0)
            finish_y(1)
            for q in range(PAIRS):
                dve.wait_ge(s_gates, q + 1)
                for j in range(NE + 1):
                    for t in range(TP):
                        m = (q * (NE + 1) + j) * 2 + t // 2
                        dve.wait_ge(s_dn, m + 1)
                        tile = q * TP + t
                        done = (q * (NE + 1) + j) * TP + t
                        if j:
                            dve.wait_ge(s_acc, done - TP + 1)
                        po = p_o[m % 3][:, (t % 2) * D:(t % 2 + 1) * D]
                        if j < NE:
                            nc.vector.scalar_tensor_tensor(x[:, tile, :], po, gates[:, tile, j:j + 1], x[:, tile, :],
                                                           ALU.mult, ALU.add).then_inc(s_acc, 1)
                        else:
                            nc.vector.tensor_tensor(x[:, tile, :], x[:, tile, :], po, ALU.add).then_inc(s_acc, 1)
                    if q == 0:
                        if j in (1, 2):
                            residual(1, j - 1)
                        if j == 2:
                            norm(1)
                        if j == 3:
                            norm_scale(1)
                        if j == 7:
                            top2(1)
                        if j == 8:
                            gate(1)
                    if q == 1 and j == 1:
                        gatesT_out(1)

        @block.tensor
        def _(pe):
            def transpose(o, i):
                n = i.shape[0]
                return nc.tensor.transpose(o, i, ident[0:n, 0:n])

            pe.wait_ge(k_ident, 1)
            for q in range(PAIRS):
                pe.wait_ge(l_ctx[q], 16)
                for t in range(TP):
                    last = transpose(p_b[q][:, t * P:(t + 1) * P], ctx_nat[:, q * TP + t, :])
                last.then_inc(t_ctx, 1)
                if q == 0:
                    for c in range(CH):
                        for k in range(DC):
                            pe.wait_ge(s_taps, c * DC + k + 1)
                            last = transpose(p_y[c][:, k * P:(k + 1) * P], w_taps[:, c, k, :])
                        last.then_inc(t_taps, 1)
            pe.wait_ge(l_xp, 64)
            for c in range(CH):
                last = transpose(p_c[:, c * XR:(c + 1) * XR], xp_nat[:, c * P:(c + 1) * P])
            last.then_inc(t_xp, 1)
            pe.wait_ge(l_dt, 16)
            pe.wait_ge(l_vec, 80)
            for c in range(CH):
                transpose(p_m[:, c * P:(c + 1) * P], dt_nat[:, c, :])
            last = transpose(p_m[:, CH * P:CH * P + 3 * CH + HC], rows[:])
            last.then_inc(t_dt, 1)

            def convolve(q, c):
                pe.wait_ge(e_ctx, q + 1)
                pe.wait_ge(e_taps, 2)
                if q and c:
                    pe.wait_ge(s_xcb, c)
                for k in range(DC):
                    last = nc.tensor.matmul(conv_out(q, c)[:], w_tapsT[:, c, k, :],
                                            ctxT[:, q * BP:(q + 1) * BP, k:k + L], start=(k == 0), stop=(k == DC - 1))
                last.then_inc(s_xc, 1)

            def project(q):
                pe.wait_ge(s_u, (q + 1) * CH)
                if q == 0:
                    pe.wait_ge(e_xp, 1)
                    pe.wait_ge(e_cols, 1)
                for c in range(CH):
                    last = nc.tensor.matmul(p_m[0:XR, :], xpT[:, c, :], u[:, q, c, :], start=(c == 0), stop=(c == CH - 1))
                last.then_inc(s_xd, 1)

            def dt_project(q, c):
                pe.wait_ge(s_xdt, q + 1)
                if q == 0:
                    pe.wait_ge(e_ctx, 2)
                elif c == 0:
                    pe.wait_ge(s_rest, q + 1)
                else:
                    pe.wait_ge(s_vb, q * CH + 1)
                nc.tensor.matmul(dt_out(q, c)[:], dtT[3 * BC:XR, c, :], xdt[3 * BC:XR, :], start=True,
                                 stop=True).then_inc(s_v, 1)

            def spread(k):
                q, n = divmod(k, DS)
                if n == 0:
                    pe.wait_ge(s_bc3, 2 * (q + 1))
                    pe.wait_ge(k_sel, 3)
                if k == 0:
                    pe.wait_ge(s_vb, CH)
                if k >= 2:
                    pe.wait_ge(s_dbu, (k - 1) * CH)
                nc.tensor.matmul(p_b[n % 2][:], selector[:, n, :], bc3[:, q, :], start=True, stop=True).then_inc(s_B, 1)
                if k == 0:
                    pe.wait_ge(e_xp, 1)
                else:
                    pe.wait_ge(s_cbc, k)
                nc.tensor.matmul(p_c[:], selector[:, DS + n, :], bc3[:, q, :], start=True, stop=True).then_inc(s_C, 1)

            def sum_n(i):
                q, n, c = i // UNITS, i % UNITS // CH, i % CH
                pe.wait_ge(s_hc, i + 1)
                if n == 0 and q:
                    pe.wait_ge(s_yt, (q - 1) * CH + c + 1)
                nc.tensor.matmul(p_y[c][:], ident[:], hc[:, i % 3, :], start=(n == 0), stop=(n == DS - 1)).then_inc(s_y, 1)

            def transpose_y(q, g):
                pe.wait_ge(s_yf, (q + 1) * CH)
                if g or q:
                    pe.wait_ge(s_x2, q * TP // 2 + g)
                for h in range(2):
                    for c in range(CH):
                        last = transpose(p_m[:, h * D + c * P:h * D + (c + 1) * P],
                                         yf[:, c, (2 * g + h) * P:(2 * g + h + 1) * P])
                    last.then_inc(s_yT, 1)

            def transpose_xf(q, c):
                pe.wait_ge(s_xf, (q + 1) * TP)
                if c:
                    pe.wait_ge(s_xfTe, q * CH + c)
                for t in range(TP):
                    last = transpose(p_m[:, t * P:(t + 1) * P], xf[:, q * TP + t, c * P:(c + 1) * P])
                last.then_inc(s_xfT, 1)

            def logits(q):
                pe.wait_ge(s_xfTe, (q + 1) * CH)
                pe.wait_ge(l_gw, 16)
                for t in range(TP):
                    tok = (q * TP + t) * P
                    for c in range(CH):
                        last = nc.tensor.matmul(p_m[:, t * NE:(t + 1) * NE], xfT[:, c, tok:tok + P], gw[:, c, :],
                                                start=(c == 0), stop=(c == CH - 1))
                last.then_inc(s_lg, 1)

            def transpose_gates(q):
                pe.wait_ge(s_gates, q + 1)
                pe.wait_ge(s_lge, q + 1)
                for t in range(TP):
                    last = transpose(p_m[0:NE + 1, t * P:(t + 1) * P], gates[:, q * TP + t, :])
                last.then_inc(s_gT, 1)

            convolve(0, 0)
            convolve(0, 1)
            project(0)
            dt_project(0, 0)
            dt_project(0, 1)
            spread(0)
            spread(1)
            for q in range(PAIRS):
                for n in range(DS):
                    k = q * DS + n
                    for c in range(CH):
                        sum_n(k * CH + c)
                    if k + 2 < PAIRS * DS:
                        spread(k + 2)
                    if q == 0:
                        if n in (1, 3):
                            convolve(1, n // 2)
                        if n == 6:
                            project(1)
                        if n == 8:
                            dt_project(1, 0)
                        if n == 10:
                            dt_project(1, 1)
                    if q == 1:
                        if n == 1:
                            transpose_y(0, 0)
                        if n == 3:
                            transpose_y(0, 1)
                        if n == 8:
                            transpose_xf(0, 0)
                        if n == 9:
                            transpose_xf(0, 1)
                        if n == 11:
                            logits(0)
                        if n == 15:
                            transpose_gates(0)
            def up(q, j):
                m = q * HC + j
                if m == 0:
                    pe.wait_ge(l_up, 64)
                    pe.wait_ge(s_dbu, PAIRS * UNITS)
                if j == 0:
                    pe.wait_ge(s_xfTe, (q + 1) * CH)
                if m >= 2:
                    pe.wait_ge(s_hid, m - 1)
                for c in range(CH):
                    last = nc.tensor.matmul(p_b[m % 2][:], w_up[:, c, j, :], xfT[:, c, q * W:(q + 1) * W], start=(c == 0),
                                            stop=(c == CH - 1))
                last.then_inc(s_up, 1)

            def down(q, j):
                if q == 0 and j == 0:
                    pe.wait_ge(l_dn, 32)
                    pe.wait_ge(s_h, PAIRS * UNITS)
                    pe.wait_ge(s_cbc, PAIRS * DS)
                chunks = [j] if j < NE else list(range(NE, HC))
                pe.wait_ge(s_hid, q * HC + chunks[-1] + 1)
                if j == NE:
                    pe.wait_ge(l_b2, 32)
                    pe.wait_ge(s_gTe, q + 1)
                for g in range(2):
                    m = (q * (NE + 1) + j) * 2 + g
                    if m >= 3:
                        pe.wait_ge(s_acc, 2 * (m - 2))
                    for h in range(2):
                        t = 2 * g + h
                        po = p_o[m % 3][:, h * D:(h + 1) * D]
                        if j == NE:
                            nc.tensor.matmul(po, gatesT[:, (q * TP + t) * P:(q * TP + t + 1) * P], b2a[:], start=True, stop=False)
                        for jj in chunks:
                            last = nc.tensor.matmul(po, hid[:, (q * HC + jj) % 3, t * P:(t + 1) * P], w_dn[:, jj, :],
                                                    start=(j < NE), stop=(jj == chunks[-1]))
                    last.then_inc(s_dn, 1)

            def experts_of(q):
                up(q, 0)
                for j in range(NE):
                    up(q, j + 1)
                    down(q, j)
                    if q == 0:
                        if j in (1, 2):
                            transpose_y(1, j - 1)
                        if j in (4, 5):
                            transpose_xf(1, j - 4)
                        if j == 6:
                            logits(1)
                    if q == 1 and j == 1:
                        transpose_gates(1)
                for j in range(NE + 1, HC):
                    up(q, j)
                down(q, NE)

            experts_of(0)
            experts_of(1)


_INS = ['x', 'ctx_1024', 'L0_xattn_in_proj_w', 'L0_xattn_conv_w', 'L0_xattn_conv_b', 'L0_xattn_x_proj_w',
        'L0_xattn_dt_proj_w', 'L0_xattn_dt_proj_b', 'L0_xattn_A_log', 'L0_xattn_D', 'L0_ffn_gate_w', 'L0_ffn_w1',
        'L0_ffn_b1', 'L0_ffn_w2', 'L0_ffn_b2', 'L0_ffn_shared_w1', 'L0_ffn_shared_b1', 'L0_ffn_shared_w2',
        'L0_ffn_shared_b2']
_OUTS = [((4, 256, 256), 'float32')]


def kernel(**inputs):
    import numpy as _np
    import concourse.bacc as _bacc
    from concourse import mybir as _mybir
    from concourse.bass_utils import run_bass_kernel_spmd as _run

    nc = _bacc.Bacc("TRN2", target_bir_lowering=False, num_devices=1)
    arrays, args = {}, []
    for name in _INS:
        a = _np.ascontiguousarray(inputs[name])
        arrays[f"in_{name}_dram"] = a
        args.append(nc.dram_tensor(f"in_{name}_dram", a.shape, _mybir.dt.from_np(a.dtype), kind="ExternalInput").ap())
    for i, (shape, dtype) in enumerate(_OUTS):
        dt = _mybir.dt.from_np(_np.dtype(dtype))
        args.append(nc.dram_tensor(f"out_{i}_dram", shape, dt, kind="ExternalOutput").ap())
    mamba_xattn_moe_ffn(nc, *args)
    r = _run(nc, [arrays], core_ids=[0])
    got = tuple(r.results[0][f"out_{i}_dram"] for i in range(len(_OUTS)))
    return got[0]
```

```python
from contextlib import ExitStack

import concourse.bass as bass
from concourse import mybir

F32 = mybir.dt.float32
F32R = mybir.dt.float32r
BF16 = mybir.dt.bfloat16
U32 = mybir.dt.uint32
ALU = mybir.AluOpType
ACT = mybir.ActivationFunctionType

P = 128
LN_EPS = 1e-5


def mamba_xattn_moe_ffn(
    nc: bass.Bass,
    x_in: bass.AP,
    ctx_in: bass.AP,
    in_proj_w: bass.AP,
    conv_w: bass.AP,
    conv_b: bass.AP,
    x_proj_w: bass.AP,
    dt_proj_w: bass.AP,
    dt_proj_b: bass.AP,
    A_log: bass.AP,
    D_skip: bass.AP,
    gate_w: bass.AP,
    w1: bass.AP,
    b1: bass.AP,
    w2: bass.AP,
    b2: bass.AP,
    shared_w1: bass.AP,
    shared_b1: bass.AP,
    shared_w2: bass.AP,
    shared_b2: bass.AP,
    out: bass.AP,
):
    B, L, DI = x_in.shape
    DM = ctx_in.shape[2]
    DC = conv_w.shape[1]
    DR = dt_proj_w.shape[1]
    DS = A_log.shape[1]
    NE, D, H = w1.shape
    CH = DI // P
    LT = L // P
    T = B * LT
    PAIRS = B // 2
    BP = B // PAIRS
    W = BP * L
    TP = T // PAIRS
    UNITS = DS * CH
    SH = shared_w1.shape[1]
    HC = NE + SH // P
    PAD = DC - 1
    LP = L + PAD + 1
    assert DM == P and D == DI and H == P and W == 512 and CH == 2 and LT == 2
    BC = 2 * DS
    assert BC == 32
    XR = 3 * BC + DR

    with ExitStack() as ctx:

        def sb(name, shape, dt=F32):
            return ctx.enter_context(nc.sbuf_tensor(name, shape, dt))

        def sem(name):
            return ctx.enter_context(nc.semaphore(name))

        NA, NC, NH, NP = 4, 3, 4, 5
        NHID = 4

        x = sb("x", [P, T, D])
        ctx_nat = sb("ctx_nat", [P, T, DM])
        ctxT = sb("ctxT", [P, 2, B, LP], F32R)
        w_in = sb("w_in", [P, CH, DM])
        cw = sb("cw", [P, CH, DC])
        rows = sb("rows", [3 * CH + HC, P])
        cols = sb("cols", [P, 3 * CH + HC])
        cb = cols[:, 0:CH]
        dtb = cols[:, CH:2 * CH]
        dsk = cols[:, 2 * CH:3 * CH]
        b1T = cols[:, 3 * CH:3 * CH + HC]
        alog = sb("alog", [P, CH, DS])
        aneg = sb("aneg", [P, CH, DS])
        w_taps = sb("w_taps", [P, CH, DC, DM])
        w_tapsT = sb("w_tapsT", [P, 2, CH, DC, P], F32R)
        xp_nat = sb("xp_nat", [DR + BC, DI])
        xpT = sb("xpT", [P, CH, XR])
        dt_nat = sb("dt_nat", [P, CH, P])
        dtT = sb("dtT", [P, CH, P])
        ident = sb("ident", [P, P])
        selector = sb("selector", [3 * BC, BC], BF16)
        u = sb("u", [P, PAIRS, CH, W])
        sz = sb("sz", [P, PAIRS, CH, W])
        minus_half = sb("minus_half", [P, T])
        zstat = sb("zstat", [P, T, 6])
        zmv = sb("zmv", [P, T, 2])
        zrstd = sb("zrstd", [P, T])
        znmr = sb("znmr", [P, T])
        xdt = sb("xdt", [P, W])
        bc3 = sb("bc3", [3 * BC, PAIRS, W], BF16)
        bc_rest = sb("bc_rest", [3 * BC, W])
        bc_mid = sb("bc_mid", [3 * BC, W], BF16)
        vpos = sb("vpos", [P, CH, W])
        sp = sb("sp", [P, CH, W])
        delta = sb("delta", [P, PAIRS, CH, W])
        du = sb("du", [P, PAIRS, CH, W])
        decay = sb("decay", [P, NA, W])
        c_bc = sb("c_bc", [P, NC, W])
        dbu = sb("dbu", [P, 3, W])
        hst = sb("hst", [P, NH, W])
        hc = sb("hc", [P, NP, W])
        yt = w_taps[:].rearrange("p c k d -> p c (k d)")
        nstat = sb("nstat", [P, T, 6])
        nmv = sb("nmv", [P, T, 2])
        nrstd = sb("nrstd", [P, T])
        xf = ctx_nat[:].rearrange("p (t r) d -> p t (r d)", r=2)
        xfT = sb("xfT", [P, 2, CH, T * P], F32R)
        gw = sb("gw", [P, CH, NE])
        gws = sb("gws", [P, 2, CH, NE], F32R)
        lg = sb("lg", [P, T, NE])
        mx = sb("mx", [P, T, 8])
        mi = sb("mi", [P, T, 8], U32)
        mif = sb("mif", [P, T, 2])
        gd = sb("gd", [P, T])
        ge = sb("ge", [P, T])
        gs = sb("gs", [P, T])
        g12 = sb("g12", [P, T, 2])
        experts = sb("experts", [P, NE])
        hot = sb("hot", [P, T, 2, NE])
        gates = sb("gates", [P, T, NE + 1])
        gatesT = sb("gatesT", [NE + 1, T * P])
        b2a = sb("b2a", [NE + 1, D])
        w_up = sb("w_up", [P, CH, HC, H])
        w_dn = sb("w_dn", [P, HC, D])
        w_ups = sb("w_ups", [P, 2, CH, HC, H], F32R)
        w_dns = sb("w_dns", [P, 2, HC, D], F32R)
        hid32 = sp
        hid_high = ctxT[:].rearrange("p r b l -> p (r b l)")[:, 0:NHID * W].rearrange("p (s w) -> p s w", w=W)
        hid_low = w_tapsT[:].rearrange("p r c k e -> p (r c) (k e)")

        bank = [ctx.enter_context(nc.psum_tensor(f"bank{i}", [P, 512], F32)) for i in range(8)]
        p_b = [bank[0], bank[1]]
        p_c = [bank[2], bank[3]]
        p_sum = [[bank[5], bank[6]], [bank[4], bank[5]]]
        p_m = bank[7]
        p_o = [bank[2], bank[3], bank[6]]

        l_ctx = [sem(f"l_ctx{q}") for q in range(PAIRS)]
        l_win = sem("l_win")
        l_xp = sem("l_xp")
        l_dt = sem("l_dt")
        l_vec = sem("l_vec")
        l_alog = sem("l_alog")
        l_x = [sem(f"l_x{q}") for q in range(PAIRS)]
        l_gw = sem("l_gw")
        l_b2 = sem("l_b2")
        l_up = sem("l_up")
        l_dn = sem("l_dn")
        k_ident = sem("k_ident")
        k_sel = sem("k_sel")
        k_pool = sem("k_pool")
        k_warm = sem("k_warm")
        k_const = sem("k_const")
        k_zero = sem("k_zero")
        s_taps = sem("s_taps")
        t_taps = sem("t_taps")
        e_taps = sem("e_taps")
        t_ctx = sem("t_ctx")
        h_ctx = sem("h_ctx")
        h_taps = sem("h_taps")
        h_gw = sem("h_gw")
        e_gw = sem("e_gw")
        h_up = sem("h_up")
        h_dn = sem("h_dn")
        e_up = sem("e_up")
        e_dn = sem("e_dn")
        h_xfT = sem("h_xfT")
        s_hidh = sem("s_hidh")
        s_hid32 = sem("s_hid32")
        e_ctx = sem("e_ctx")
        t_xp = sem("t_xp")
        e_xp = sem("e_xp")
        t_dt = sem("t_dt")
        e_dt = sem("e_dt")
        e_cols = sem("e_cols")
        s_aneg = sem("s_aneg")
        s_xc = sem("s_xc")
        s_u = sem("s_u")
        s_zst = sem("s_zst")
        s_zmv = sem("s_zmv")
        s_zr = sem("s_zr")
        s_z = sem("s_z")
        s_sz = sem("s_sz")
        s_xd = sem("s_xd")
        s_xdt = sem("s_xdt")
        s_hi = sem("s_hi")
        s_rest = sem("s_rest")
        s_mid = sem("s_mid")
        s_bc3 = sem("s_bc3")
        s_v = sem("s_v")
        s_abs = sem("s_abs")
        s_vpos = sem("s_vpos")
        s_ex = sem("s_ex")
        s_ln = sem("s_ln")
        s_delta = sem("s_delta")
        s_du = sem("s_du")
        s_B = sem("s_B")
        s_C = sem("s_C")
        s_cbc = sem("s_cbc")
        s_decay = sem("s_decay")
        s_dbu = sem("s_dbu")
        s_h = sem("s_h")
        s_hc = sem("s_hc")
        s_y = sem("s_y")
        s_yt = sem("s_yt")
        s_yf = sem("s_yf")
        s_yT = sem("s_yT")
        s_x2 = sem("s_x2")
        s_nst = sem("s_nst")
        s_nmv = sem("s_nmv")
        s_nr = sem("s_nr")
        s_xf = sem("s_xf")
        s_xfT = sem("s_xfT")
        s_xfTe = sem("s_xfTe")
        s_lg = sem("s_lg")
        s_lge = sem("s_lge")
        s_mx = sem("s_mx")
        s_mi = sem("s_mi")
        s_gd = sem("s_gd")
        s_ge = sem("s_ge")
        s_g = sem("s_g")
        s_gates = sem("s_gates")
        s_gT = sem("s_gT")
        s_gTe = sem("s_gTe")
        s_up = sem("s_up")
        s_hid = sem("s_hid")
        s_dn = sem("s_dn")
        s_acc = sem("s_acc")
        s_out = sem("s_out")

        x_tok = x_in.rearrange("b (t p) d -> p (b t) d", p=P)
        out_tok = out.rearrange("b (t p) d -> p (b t) d", p=P)
        ctx_tok = ctx_in.rearrange("b (t p) d -> p (b t) d", p=P)

        def as_rows(v):
            return v.rearrange("(c p) -> c p", p=P)

        def chans(v):
            return v.rearrange("(c p) k -> p c k", p=P)

        def batches(ap):
            return ap.rearrange("p (b l) -> p b l", b=BP)

        def conv_out(q, c):
            return p_sum[0][c] if q == 0 else (bank[4], p_m)[c]

        def ctx_out(q):
            return (p_b[0], p_c[1])[q]

        def dt_out(q, c):
            return p_b[c] if q == 0 else (bank[4], p_m)[c]

        def misc(q, g):
            return p_m if g == 0 else (bank[6], bank[4])[q]

        def groups_with(m):
            q, j = divmod(m, HC)
            return q * (NE + 1) + min(j, NE) + 1

        w_blocks = [(w_up[:, c, j:j + 5], w_ups[:, 0, c, j:j + 5], w_ups[:, 1, c, j:j + 5]) for j in (0, 5) for c in range(CH)]
        w_blocks += [(w_dn[:, j:j + 2], w_dns[:, 0, j:j + 2], w_dns[:, 1, j:j + 2]) for j in range(0, HC, 2)]

        UPS = 2 * CH

        def weights_low(engine, queue, k):
            raw, high, low = w_blocks[k]
            queue.wait_ge(h_up if k < UPS else h_dn, k + 1 if k < UPS else k + 1 - UPS)
            engine.tensor_tensor(low, raw, high.bitcast(F32), ALU.subtract).then_inc(e_up if k < UPS else e_dn, 1)

        block = ctx.enter_context(nc.Block())

        @block.sync
        def _(sp_):
            def load(dst, src, done):
                sp_.dma_start(dst, src).then_inc(done, 16)

            def load_ctx(q):
                load(ctx_nat[:, q * TP:(q + 1) * TP, :], ctx_tok[:, q * TP:(q + 1) * TP, :], l_ctx[q])

            load_ctx(0)
            load(xp_nat[:], x_proj_w, l_xp)
            for r, v in enumerate((conv_b, dt_proj_b, D_skip, shared_b1)):
                at = r * CH if r < 3 else 3 * CH + NE
                load(rows[at:at + CH, :], as_rows(v), l_vec)
            load(rows[3 * CH:3 * CH + NE, :], b1, l_vec)
            sp_.wait_ge(k_zero, 1)
            load(dt_nat[:, :, 3 * BC:XR], chans(dt_proj_w), l_dt)
            load(x[:, 0:TP], x_tok[:, 0:TP], l_x[0])
            load_ctx(1)
            load(x[:, TP:T], x_tok[:, TP:T], l_x[1])
            load(alog[:], chans(A_log), l_alog)
            load(gw[:], chans(gate_w), l_gw)
            for c in range(CH):
                load(w_up[:, c, 0:NE, :], w1[:, c * P:(c + 1) * P, :].rearrange("e p h -> p e h"), l_up)
                load(w_up[:, c, NE:HC, :], shared_w1[c * P:(c + 1) * P, :].rearrange("p (j h) -> p j h", h=H), l_up)
            load(w_dn[:, 0:NE, :], w2.rearrange("e p d -> p e d"), l_dn)
            load(w_dn[:, NE:HC, :], shared_w2.rearrange("(j p) d -> p j d", p=P), l_dn)
            load(b2a[0:NE, :], b2, l_b2)
            load(b2a[NE:NE + 1, :], shared_b2.rearrange("(a d) -> a d", a=1), l_b2)
            for q in range(PAIRS):
                for t in range(TP):
                    sp_.wait_ge(s_acc, q * TP * (NE + 1) + TP * NE + t + 1)
                    sp_.dma_start(out_tok[:, q * TP + t, :], x[:, q * TP + t, :]).then_inc(s_out, 16)
            sp_.wait_ge(s_out, 16 * T)

        @block.gpsimd
        def _(pool):
            nc.gpsimd.memset(ident[:], 0.0).then_inc(k_pool, 1)
            pool.wait_ge(k_pool, 1)
            nc.gpsimd.affine_select(out=ident[:], in_=ident[:], compare_op=ALU.not_equal, fill=1.0, base=0,
                                    pattern=[[-1, P]], channel_multiplier=1).then_inc(k_ident, 1)
            nc.gpsimd.memset(ctxT[:, :, :, 0:PAD].bitcast(F32), 0.0).then_inc(k_const, 1)
            nc.gpsimd.memset(selector[:], 0.0).then_inc(k_pool, 1)
            pool.wait_ge(k_pool, 2)
            for r in range(3):
                nc.gpsimd.affine_select(out=selector[:], in_=selector[:], compare_op=ALU.not_equal, fill=1.0,
                                        base=-BC * r, pattern=[[-1, BC]], channel_multiplier=1).then_inc(k_sel, 1)
                pool.wait_ge(k_sel, r + 1)
            nc.gpsimd.memset(minus_half[:], -0.5).then_inc(k_const, 1)
            nc.gpsimd.iota(experts[:], [[1, NE]], base=0, channel_multiplier=0,
                           allow_small_or_imprecise_dtypes=True).then_inc(k_const, 1)
            nc.gpsimd.memset(gates[:, :, NE:NE + 1], 1.0).then_inc(k_const, 1)
            nc.gpsimd.memset(decay[:].rearrange("p s (b l) -> p s b l", b=BP)[:, :, :, 0:1], 0.0).then_inc(k_const, 1)
            pool.wait_ge(k_const, 2)

            def rstd(o, var, steps, done):
                nc.gpsimd.tensor_scalar(o, var, LN_EPS, None, ALU.add).then_inc(k_pool, 1)
                pool.wait_ge(k_pool, steps)
                nc.gpsimd.tensor_tensor(o, o, minus_half[:, 0:var.shape[1]], ALU.pow).then_inc(done, 1)

            for q in range(PAIRS):
                pool.wait_ge(s_zmv, (q + 1) * TP)
                rstd(zrstd[:, q * TP:(q + 1) * TP], zmv[:, q * TP:(q + 1) * TP, 1], 3 + q, s_zr)
            for k in range(UPS):
                weights_low(nc.gpsimd, pool, k)
            pool.wait_ge(s_aneg, 1)
            nc.gpsimd.tensor_scalar(aneg[:], aneg[:], -1.0, None, ALU.mult).then_inc(s_aneg, 1)

            def token_rstd(q):
                a, b = q * TP, (q + 1) * TP
                pool.wait_ge(s_nmv, b)
                rstd(nrstd[:, a:b], nmv[:, a:b, 1], 3 + PAIRS + q, s_nr)

            for q in range(PAIRS):
                for n in range(DS):
                    if q == 1 and n == 5:
                        token_rstd(0)
                    k = q * DS + n
                    for c in range(CH):
                        i = k * CH + c
                        pool.wait_ge(s_h, i + 1)
                        pool.wait_ge(s_cbc, k + 1)
                        if i >= NP:
                            pool.wait_ge(s_y, i - NP + 1)
                        nc.gpsimd.tensor_tensor(hc[:, i % NP, :], hst[:, i % NH, :], c_bc[:, k % NC, :], ALU.mult).then_inc(s_hc, 1)
            for m in range(PAIRS * HC):
                if m == 3:
                    token_rstd(1)
                pool.wait_ge(s_hid32, m + 1)
                if m >= NHID:
                    pool.wait_ge(s_dn, 2 * groups_with(m - NHID))
                nc.gpsimd.tensor_tensor(hid_low[:, m % NHID, :], hid32[:, m % 2, :], hid_high[:, m % NHID, :].bitcast(F32),
                                        ALU.subtract).then_inc(s_hid, 1)

        @block.scalar
        def _(act):
            act.dma_start(w_in[:], chans(in_proj_w)).then_inc(l_win, 16)
            act.dma_start(cw[:], chans(conv_w)).then_inc(l_win, 16)
            nc.scalar.preload_act_table_set("silu_and_others")
            act.wait_ge(k_const, 1)

            def ctx_high(q):
                act.wait_ge(t_ctx, q + 1)
                nc.scalar.copy(ctxT[:, 0, q * BP:(q + 1) * BP, PAD:PAD + L], batches(ctx_out(q)[:])).then_inc(h_ctx, 1)

            ctx_high(0)
            for c in range(CH):
                act.wait_ge(t_taps, c + 1)
                nc.scalar.copy(w_tapsT[:, 0, c], p_sum[0][c][:].rearrange("p (k d) -> p k d", k=DC)).then_inc(h_taps, 1)
            ctx_high(1)

            def silu_u(q, c):
                act.wait_ge(s_xc, q * CH + c + 1)
                act.wait_ge(e_cols, 1)
                nc.scalar.activation(u[:, q, c, :], conv_out(q, c)[:], ACT.Silu, bias=cb[:, c:c + 1]).then_inc(s_u, 1)

            def silu_z(t):
                q = t // TP
                b, c = divmod(t - q * TP, LT)
                nc.scalar.activation(sz[:, q, c, b * L:(b + 1) * L], x[:, t, :], ACT.Silu, scale=zrstd[:, t:t + 1],
                                     bias=znmr[:, t:t + 1]).then_inc(s_sz, 1)

            def dt_rows(q):
                act.wait_ge(s_xd, q + 1)
                if q:
                    act.wait_ge(s_v, q * CH)
                nc.scalar.copy(xdt[3 * BC:XR, :], p_m[3 * BC:XR, :]).then_inc(s_xdt, 1)

            def softplus_abs(q, c):
                act.wait_ge(s_v, q * CH + c + 1)
                if q:
                    act.wait_ge(s_delta, c + 1)
                nc.scalar.activation(sp[:, c, :], dt_out(q, c)[:], ACT.Abs, bias=dtb[:, c:c + 1]).then_inc(s_abs, 1)

            def softplus_log(q, c):
                act.wait_ge(s_abs, q * CH + c + 1)
                nc.scalar.activation(sp[:, c, :], sp[:, c, :], ACT.Exp, scale=-1.0).then_inc(s_ex, 1)
                act.wait_ge(s_ex, q * CH + c + 1)
                nc.scalar.activation(sp[:, c, :], sp[:, c, :], ACT.Ln, bias=1.0).then_inc(s_ln, 1)

            def weights_high(k):
                raw, high, low = w_blocks[k]
                act.wait_ge(l_dn, 32)
                nc.scalar.copy(high, raw).then_inc(h_dn, 1)

            def gate_exp(q):
                act.wait_ge(s_gd, q + 1)
                nc.scalar.activation(ge[:, q * TP:(q + 1) * TP], gd[:, q * TP:(q + 1) * TP], ACT.Exp).then_inc(s_ge, 1)

            def spread_C(q, n):
                k = q * DS + n
                act.wait_ge(s_C, k + 1)
                if k >= NC:
                    act.wait_ge(s_hc, (k - NC + 1) * CH)
                nc.scalar.copy(c_bc[:, k % NC, :], p_c[k % 2][:]).then_inc(s_cbc, 1)

            def xfT_out(q, c):
                act.wait_ge(s_xfT, q * CH + c + 1)
                nc.scalar.copy(xfT[:, 0, c, q * W:(q + 1) * W], misc(q, c)[:]).then_inc(h_xfT, 1)

            silu_u(0, 0)
            silu_u(0, 1)
            act.wait_ge(s_z, 1)
            for t in range(TP):
                silu_z(t)
            dt_rows(0)
            nc.scalar.preload_act_table_set("natural_log_exp_and_others")
            act.wait_ge(l_alog, 16)
            nc.scalar.activation(aneg[:], alog[:], ACT.Exp).then_inc(s_aneg, 1)
            softplus_abs(0, 0)
            softplus_log(0, 0)
            softplus_abs(0, 1)
            softplus_log(0, 1)
            act.wait_ge(s_aneg, 2)
            act.wait_ge(k_const, 5)
            for q in range(PAIRS):
                for n in range(DS):
                    for c in range(CH):
                        i = (q * DS + n) * CH + c
                        if n == 0:
                            act.wait_ge(s_delta, q * CH + c + 1)
                        if i >= NA:
                            act.wait_ge(s_h, i - NA + 1)
                        nc.scalar.activation(batches(decay[:, i % NA, :])[:, :, 1:L], batches(delta[:, q, c, :])[:, :, 1:L],
                                             ACT.Exp, scale=aneg[:, c, n:n + 1]).then_inc(s_decay, 1)
                        if c == 0:
                            spread_C(q, n)
                    if q == 0 and n == 2:
                        nc.scalar.preload_act_table_set("silu_and_others")
                        silu_u(1, 0)
                        silu_u(1, 1)
                        nc.scalar.preload_act_table_set("natural_log_exp_and_others")
                    if q == 0 and n == 7:
                        dt_rows(1)
                    if q == 0 and n in (10, 11):
                        softplus_abs(1, n - 10)
                    if q == 0 and n in (12, 13):
                        softplus_log(1, n - 12)
                    if q == 1 and n in (2, 3, 4, 5, 6):
                        weights_high(UPS + n - 2)
                    if q == 1 and n in (9, 10):
                        xfT_out(0, n - 9)
                    if q == 1 and n == 14:
                        gate_exp(0)
            for t in range(TP, T):
                silu_z(t)
            act.wait_ge(s_delta, PAIRS * CH)
            for q in range(PAIRS):
                for j in range(HC):
                    m = q * HC + j
                    act.wait_ge(s_up, m + 1)
                    if m >= NHID:
                        act.wait_ge(s_dn, 2 * groups_with(m - NHID))
                    nc.scalar.activation(hid_high[:, m % NHID, :], p_b[m % 2][:], ACT.Gelu, bias=b1T[:, j:j + 1]).then_inc(s_hidh, 1)
                    if m >= 2:
                        act.wait_ge(s_hid, m - 1)
                    nc.scalar.activation(hid32[:, m % 2, :], p_b[m % 2][:], ACT.Gelu, bias=b1T[:, j:j + 1]).then_inc(s_hid32, 1)
                    if q == 0 and j in (5, 6):
                        xfT_out(1, j - 5)
                    if q == 0 and j == 8:
                        gate_exp(1)

        @block.vector
        def _(dve):
            nc.vector.memset(dt_nat[:], 0.0).then_inc(k_zero, 1)
            dve.wait_ge(l_win, 32)
            for c in range(CH):
                for k in range(DC):
                    nc.vector.tensor_scalar(w_taps[:, c, k, :], w_in[:, c, :], cw[:, c, k:k + 1], None, ALU.mult).then_inc(s_taps, 1)

            def ctx_low(q):
                dve.wait_ge(h_ctx, q + 1)
                ours = slice(q * BP, (q + 1) * BP)
                nc.vector.tensor_tensor(ctxT[:, 1, ours, PAD:PAD + L], batches(ctx_out(q)[:]),
                                        ctxT[:, 0, ours, PAD:PAD + L].bitcast(F32), ALU.subtract).then_inc(e_ctx, 1)

            ctx_low(0)
            for c in range(CH):
                dve.wait_ge(h_taps, c + 1)
                nc.vector.tensor_tensor(w_tapsT[:, 1, c], p_sum[0][c][:].rearrange("p (k d) -> p k d", k=DC),
                                        w_tapsT[:, 0, c].bitcast(F32), ALU.subtract).then_inc(e_taps, 1)
            dve.wait_ge(t_xp, 1)
            xpt = p_c[0][:, 0:CH * (DR + BC)].rearrange("p (c r) -> p c r", c=CH)
            for r in range(3):
                nc.vector.tensor_copy(xpT[:, :, r * BC:(r + 1) * BC], xpt[:, :, DR:DR + BC]).then_inc(e_xp, 1)
            nc.vector.tensor_copy(xpT[:, :, 3 * BC:XR], xpt[:, :, 0:DR]).then_inc(e_xp, 1)
            dve.wait_ge(t_dt, 1)
            nc.vector.tensor_copy(dtT[:], p_m[:, 0:CH * P].rearrange("p (c e) -> p c e", c=CH)).then_inc(e_dt, 1)
            nc.vector.tensor_copy(cols[:], p_m[:, CH * P:CH * P + 3 * CH + HC]).then_inc(e_cols, 1)
            ctx_low(1)

            def norm_z(q):
                a, b = q * TP, (q + 1) * TP
                dve.wait_ge(l_x[q], 16)
                for t in range(a, b):
                    nc.vector.bn_stats(zstat[:, t, :], x[:, t, :]).then_inc(s_zst, 1)
                for t in range(a, b):
                    dve.wait_ge(s_zst, t + 1)
                    nc.vector.bn_aggr(zmv[:, t, :], zstat[:, t, :]).then_inc(s_zmv, 1)

            def norm_z_offset(q):
                a, b = q * TP, (q + 1) * TP
                dve.wait_ge(s_zr, q + 1)
                nc.vector.scalar_tensor_tensor(znmr[:, a:b], zmv[:, a:b, 0], -1.0, zrstd[:, a:b], ALU.mult,
                                               ALU.mult).then_inc(s_z, 1)

            def split_bc(q):
                dve.wait_ge(s_xd, q + 1)
                bcq = bc3[:, q, :]
                nc.vector.tensor_copy(bcq, p_m[0:3 * BC, :]).then_inc(s_hi, 1)
                dve.wait_ge(s_hi, q + 1)
                if q:
                    dve.wait_ge(s_bc3, 2 * q)
                nc.vector.tensor_tensor(bc_rest[:], p_m[0:3 * BC, :], bcq, ALU.subtract).then_inc(s_rest, 1)
                dve.wait_ge(s_rest, q + 1)
                nc.vector.tensor_copy(bc_mid[2 * BC:3 * BC, :], bc_rest[2 * BC:3 * BC, :]).then_inc(s_mid, 1)
                nc.vector.tensor_copy(bc3[BC:2 * BC, q, :], bc_rest[BC:2 * BC, :]).then_inc(s_bc3, 1)
                dve.wait_ge(s_mid, q + 1)
                nc.vector.tensor_tensor(bc3[2 * BC:3 * BC, q, :], bc_rest[2 * BC:3 * BC, :], bc_mid[2 * BC:3 * BC, :],
                                        ALU.subtract).then_inc(s_bc3, 1)

            def positive(q, c):
                dve.wait_ge(s_abs, q * CH + c + 1)
                nc.vector.tensor_scalar(vpos[:, c, :], dt_out(q, c)[:], dtb[:, c:c + 1], 0.0, ALU.add, ALU.max).then_inc(s_vpos, 1)

            def softplus_end(q, c):
                dve.wait_ge(s_ln, q * CH + c + 1)
                dve.wait_ge(s_vpos, q * CH + c + 1)
                nc.vector.tensor_tensor(delta[:, q, c, :], vpos[:, c, :], sp[:, c, :], ALU.add).then_inc(s_delta, 1)
                dve.wait_ge(s_delta, q * CH + c + 1)
                nc.vector.tensor_tensor(du[:, q, c, :], delta[:, q, c, :], u[:, q, c, :], ALU.mult).then_inc(s_du, 1)

            def drive(i):
                q, n, c = i // UNITS, i % UNITS // CH, i % CH
                if n == 0:
                    dve.wait_ge(s_du, q * CH + c + 1)
                dve.wait_ge(s_B, q * DS + n + 1)
                if i >= 3:
                    dve.wait_ge(s_h, i - 2)
                nc.vector.tensor_tensor(dbu[:, i % 3, :], du[:, q, c, :], p_b[n % 2][:], ALU.mult).then_inc(s_dbu, 1)

            def scan(i):
                dve.wait_ge(s_dbu, i + 1)
                dve.wait_ge(s_decay, i + 1)
                if i >= NH:
                    dve.wait_ge(s_hc, i - NH + 1)
                nc.vector.tensor_tensor_scan(hst[:, i % NH, :], decay[:, i % NA, :], dbu[:, i % 3, :], 0.0, ALU.mult,
                                             ALU.add).then_inc(s_h, 1)

            def finish_y(q):
                dve.wait_ge(s_y, (q + 1) * UNITS)
                dve.wait_ge(s_sz, (q + 1) * TP)
                if q:
                    dve.wait_ge(s_yT, q * TP)
                for c in range(CH):
                    nc.vector.scalar_tensor_tensor(yt[:, c, :], u[:, q, c, :], dsk[:, c:c + 1], p_sum[q][c][:], ALU.mult,
                                                   ALU.add).then_inc(s_yt, 1)
                for c in range(CH):
                    dve.wait_ge(s_yt, q * CH + c + 1)
                    nc.vector.tensor_tensor(yt[:, c, :], yt[:, c, :], sz[:, q, c, :], ALU.mult).then_inc(s_yf, 1)

            def residual(q, g):
                t = q * TP + 2 * g
                dve.wait_ge(s_yT, t + 2)
                nc.vector.tensor_tensor(x[:, t:t + 2, :], x[:, t:t + 2, :], misc(q, g)[:].rearrange("p (t d) -> p t d", t=2),
                                        ALU.add).then_inc(s_x2, 1)

            def norm(q):
                a, b = q * TP, (q + 1) * TP
                dve.wait_ge(s_x2, b // 2)
                for t in range(a, b):
                    nc.vector.bn_stats(nstat[:, t, :], x[:, t, :]).then_inc(s_nst, 1)
                for t in range(a, b):
                    dve.wait_ge(s_nst, t + 1)
                    nc.vector.bn_aggr(nmv[:, t, :], nstat[:, t, :]).then_inc(s_nmv, 1)

            def norm_scale(q):
                a, b = q * TP, (q + 1) * TP
                dve.wait_ge(s_nr, q + 1)
                for t in range(a, b):
                    nc.vector.tensor_scalar(xf[:, t - a, :], x[:, t, :], nmv[:, t, 0:1], nrstd[:, t:t + 1], ALU.subtract,
                                            ALU.mult).then_inc(s_xf, 1)

            def xfT_low(q, c):
                dve.wait_ge(h_xfT, q * CH + c + 1)
                ours = slice(q * W, (q + 1) * W)
                nc.vector.tensor_tensor(xfT[:, 1, c, ours], misc(q, c)[:], xfT[:, 0, c, ours].bitcast(F32),
                                        ALU.subtract).then_inc(s_xfTe, 1)

            def top2(q):
                a, b = q * TP, (q + 1) * TP
                dve.wait_ge(s_lg, q + 1)
                nc.vector.tensor_copy(lg[:, a:b, :], p_m[:, 0:TP * NE].rearrange("p (t e) -> p t e", t=TP)).then_inc(s_lge, 1)
                dve.wait_ge(s_lge, q + 1)
                for t in range(a, b):
                    nc.vector.max(mx[:, t, :], lg[:, t, :]).then_inc(s_mx, 1)
                for t in range(a, b):
                    dve.wait_ge(s_mx, t + 1)
                    nc.vector.max_index(mi[:, t, :], mx[:, t, :], lg[:, t, :]).then_inc(s_mi, 1)
                nc.vector.tensor_tensor(gd[:, a:b], mx[:, a:b, 1], mx[:, a:b, 0], ALU.subtract).then_inc(s_gd, 1)
                dve.wait_ge(s_mi, b)
                nc.vector.tensor_copy(mif[:, a:b, :], mi[:, a:b, 0:2]).then_inc(s_g, 1)

            def gate(q):
                a, b = q * TP, (q + 1) * TP
                g = 8 * q
                dve.wait_ge(s_ge, q + 1)
                nc.vector.tensor_scalar(gs[:, a:b], ge[:, a:b], 1.0, None, ALU.add).then_inc(s_g, 1)
                dve.wait_ge(s_g, g + 2)
                nc.vector.reciprocal(g12[:, a:b, 0], gs[:, a:b]).then_inc(s_g, 1)
                dve.wait_ge(s_g, g + 3)
                nc.vector.tensor_tensor(g12[:, a:b, 1], ge[:, a:b], g12[:, a:b, 0], ALU.mult).then_inc(s_g, 1)
                dve.wait_ge(k_const, 4)
                for r in range(2):
                    nc.vector.tensor_tensor(hot[:, a:b, r, :], experts[:].unsqueeze(1).to_broadcast([P, TP, NE]),
                                            mif[:, a:b, r:r + 1].to_broadcast([P, TP, NE]), ALU.is_equal).then_inc(s_g, 1)
                    dve.wait_ge(s_g, g + 5 + r)
                for r in range(2):
                    nc.vector.tensor_tensor(hot[:, a:b, r, :], hot[:, a:b, r, :],
                                            g12[:, a:b, r:r + 1].to_broadcast([P, TP, NE]), ALU.mult).then_inc(s_g, 1)
                dve.wait_ge(s_g, g + 8)
                nc.vector.tensor_tensor(gates[:, a:b, 0:NE], hot[:, a:b, 0, :], hot[:, a:b, 1, :], ALU.add).then_inc(s_gates, 1)

            def gatesT_out(q):
                dve.wait_ge(s_gT, q + 1)
                nc.vector.tensor_copy(gatesT[:, q * W:(q + 1) * W], p_m[0:NE + 1, :]).then_inc(s_gTe, 1)

            norm_z(0)
            norm_z(1)
            norm_z_offset(0)
            dve.wait_ge(l_gw, 16)
            nc.vector.tensor_copy(gws[:, 0], gw[:]).then_inc(h_gw, 1)
            dve.wait_ge(h_gw, 1)
            nc.vector.tensor_tensor(gws[:, 1], gw[:], gws[:, 0].bitcast(F32), ALU.subtract).then_inc(e_gw, 1)
            norm_z_offset(1)
            split_bc(0)
            dve.wait_ge(l_up, 64)
            for raw, high, low in w_blocks[0:UPS]:
                nc.vector.tensor_copy(high, raw).then_inc(h_up, 1)
            for c in range(CH):
                positive(0, c)
            softplus_end(0, 0)
            drive(0)
            softplus_end(0, 1)
            for q in range(PAIRS):
                for n in range(DS):
                    for c in range(CH):
                        i = (q * DS + n) * CH + c
                        if i + 1 < PAIRS * UNITS:
                            drive(i + 1)
                        scan(i)
                    if q == 0:
                        if n == 6:
                            split_bc(1)
                        if n in (9, 10):
                            positive(1, n - 9)
                        if n in (11, 12):
                            softplus_end(1, n - 11)
                    if q == 1:
                        if n == 1:
                            finish_y(0)
                        if n == 3:
                            residual(0, 0)
                        if n == 4:
                            residual(0, 1)
                            norm(0)
                        if n == 6:
                            norm_scale(0)
                        if n in (8, 9):
                            xfT_low(0, n - 8)
                        if n == 11:
                            top2(0)
                        if n == 13:
                            gate(0)
                        if n == 15:
                            gatesT_out(0)
            for k in range(UPS, len(w_blocks)):
                weights_low(nc.vector, dve, k)
            finish_y(1)
            for q in range(PAIRS):
                dve.wait_ge(s_gates, q + 1)
                for j in range(NE + 1):
                    for t in range(TP):
                        m = (q * (NE + 1) + j) * 2 + t // 2
                        dve.wait_ge(s_dn, m + 1)
                        tile = q * TP + t
                        done = (q * (NE + 1) + j) * TP + t
                        if j:
                            dve.wait_ge(s_acc, done - TP + 1)
                        po = p_o[m % 3][:, (t % 2) * D:(t % 2 + 1) * D]
                        if j < NE:
                            nc.vector.scalar_tensor_tensor(x[:, tile, :], po, gates[:, tile, j:j + 1], x[:, tile, :],
                                                           ALU.mult, ALU.add).then_inc(s_acc, 1)
                        else:
                            nc.vector.tensor_tensor(x[:, tile, :], x[:, tile, :], po, ALU.add).then_inc(s_acc, 1)
                    if q == 0:
                        if j in (0, 1):
                            residual(1, j)
                        if j == 1:
                            norm(1)
                        if j == 2:
                            norm_scale(1)
                        if j in (4, 5):
                            xfT_low(1, j - 4)
                        if j == 6:
                            top2(1)
                        if j == 7:
                            gate(1)
                    if q == 1 and j == 1:
                        gatesT_out(1)

        @block.tensor
        def _(pe):
            def transpose(o, i):
                n = i.shape[0]
                return nc.tensor.transpose(o, i, ident[0:n, 0:n])

            def split_matmul(o, left, right, start=True, stop=True):
                nc.tensor.matmul(o, left[0], right[0], start=start, stop=False)
                nc.tensor.matmul(o, left[0], right[1], start=False, stop=False)
                return nc.tensor.matmul(o, left[1], right[0], start=False, stop=stop)

            def transpose_ctx(q):
                pe.wait_ge(l_ctx[q], 16)
                for t in range(TP):
                    last = transpose(ctx_out(q)[:, t * P:(t + 1) * P], ctx_nat[:, q * TP + t, :])
                last.then_inc(t_ctx, 1)

            pe.wait_ge(k_ident, 1)
            for _ in range(6):
                last = nc.tensor.matmul(p_m[:, 0:P], ident[:], ident[:], start=True, stop=True)
            last.then_inc(k_warm, 1)
            transpose_ctx(0)
            for c in range(CH):
                for k in range(DC):
                    pe.wait_ge(s_taps, c * DC + k + 1)
                    last = transpose(p_sum[0][c][:, k * P:(k + 1) * P], w_taps[:, c, k, :])
                last.then_inc(t_taps, 1)
            pe.wait_ge(l_xp, 16)
            for c in range(CH):
                last = transpose(p_c[0][:, c * (DR + BC):(c + 1) * (DR + BC)], xp_nat[:, c * P:(c + 1) * P])
            last.then_inc(t_xp, 1)
            pe.wait_ge(l_dt, 16)
            pe.wait_ge(l_vec, 80)
            pe.wait_ge(k_warm, 1)
            for c in range(CH):
                transpose(p_m[:, c * P:(c + 1) * P], dt_nat[:, c, :])
            transpose(p_m[:, CH * P:CH * P + 3 * CH + HC], rows[:]).then_inc(t_dt, 1)
            transpose_ctx(1)

            def convolve(q, c):
                pe.wait_ge(e_ctx, q + 1)
                pe.wait_ge(e_taps, CH)
                if q == 1 and c == 1:
                    pe.wait_ge(s_rest, 1)
                    pe.wait_ge(s_xdt, 1)
                ours = slice(q * BP, (q + 1) * BP)
                for k in range(DC):
                    last = split_matmul(conv_out(q, c)[:], [w_tapsT[:, r, c, k, :] for r in range(2)],
                                        [ctxT[:, r, ours, k:k + L] for r in range(2)], start=(k == 0), stop=(k == DC - 1))
                last.then_inc(s_xc, 1)

            def project(q):
                pe.wait_ge(s_u, (q + 1) * CH)
                if q == 0:
                    pe.wait_ge(e_xp, 4)
                    pe.wait_ge(e_cols, 1)
                for c in range(CH):
                    last = nc.tensor.matmul(p_m[0:XR, :], xpT[:, c, :], u[:, q, c, :], start=(c == 0), stop=(c == CH - 1))
                last.then_inc(s_xd, 1)

            def dt_project(q, c):
                pe.wait_ge(s_xdt, q + 1)
                if q == 1 and c == 1:
                    pe.wait_ge(s_rest, q + 1)
                nc.tensor.matmul(dt_out(q, c)[:], dtT[3 * BC:XR, c, :], xdt[3 * BC:XR, :], start=True,
                                 stop=True).then_inc(s_v, 1)

            def spread(k):
                q, n = divmod(k, DS)
                if n == 0:
                    pe.wait_ge(s_bc3, 2 * (q + 1))
                    pe.wait_ge(k_sel, 3)
                if k < 2:
                    pe.wait_ge(s_vpos, k + 1)
                else:
                    pe.wait_ge(s_dbu, (k - 1) * CH)
                nc.tensor.matmul(p_b[n % 2][:], selector[:, n:n + 1].to_broadcast([3 * BC, P]), bc3[:, q, :], start=True,
                                 stop=True).then_inc(s_B, 1)
                if k >= 2:
                    pe.wait_ge(s_cbc, k - 1)
                elif k == 0:
                    pe.wait_ge(e_xp, 4)
                else:
                    pe.wait_ge(e_ctx, 2)
                nc.tensor.matmul(p_c[k % 2][:], selector[:, DS + n:DS + n + 1].to_broadcast([3 * BC, P]), bc3[:, q, :],
                                 start=True, stop=True).then_inc(s_C, 1)

            def sum_n(i):
                q, n, c = i // UNITS, i % UNITS // CH, i % CH
                pe.wait_ge(s_hc, i + 1)
                if n == 0 and q:
                    pe.wait_ge(*((s_vpos, q * CH + 1) if c == 0 else (s_yt, 1)))
                nc.tensor.matmul(p_sum[q][c][:], ident[:], hc[:, i % NP, :], start=(n == 0), stop=(n == DS - 1)).then_inc(s_y, 1)

            def transpose_y(q, g):
                pe.wait_ge(s_yf, (q + 1) * CH)
                if q == 0:
                    pe.wait_ge(*((s_vpos, PAIRS * CH) if g == 0 else (s_yt, CH)))
                else:
                    pe.wait_ge(*((s_gTe, 1) if g == 0 else (s_yt, PAIRS * CH)))
                for h in range(2):
                    for c in range(CH):
                        last = transpose(misc(q, g)[:, h * D + c * P:h * D + (c + 1) * P],
                                         yt[:, c, (2 * g + h) * P:(2 * g + h + 1) * P])
                    last.then_inc(s_yT, 1)

            def transpose_xf(q, c):
                pe.wait_ge(s_xf, (q + 1) * TP)
                for t in range(TP):
                    last = transpose(misc(q, c)[:, t * P:(t + 1) * P], xf[:, t, c * P:(c + 1) * P])
                last.then_inc(s_xfT, 1)

            def logits(q):
                pe.wait_ge(s_xfTe, (q + 1) * CH)
                pe.wait_ge(e_gw, 1)
                for t in range(TP):
                    tok = (q * TP + t) * P
                    for c in range(CH):
                        last = split_matmul(p_m[:, t * NE:(t + 1) * NE], [xfT[:, r, c, tok:tok + P] for r in range(2)],
                                            [gws[:, r, c, :] for r in range(2)], start=(c == 0), stop=(c == CH - 1))
                last.then_inc(s_lg, 1)

            def transpose_gates(q):
                pe.wait_ge(s_gates, q + 1)
                pe.wait_ge(s_lge, q + 1)
                for t in range(TP):
                    last = transpose(p_m[0:NE + 1, t * P:(t + 1) * P], gates[:, q * TP + t, :])
                last.then_inc(s_gT, 1)

            def up(q, j):
                m = q * HC + j
                if m == 0:
                    pe.wait_ge(e_up, UPS)
                    pe.wait_ge(s_dbu, PAIRS * UNITS)
                if j == 0:
                    pe.wait_ge(s_xfTe, (q + 1) * CH)
                if m >= 2:
                    pe.wait_ge(s_hid32, m - 1)
                for c in range(CH):
                    last = split_matmul(p_b[m % 2][:], [w_ups[:, r, c, j, :] for r in range(2)],
                                        [xfT[:, r, c, q * W:(q + 1) * W] for r in range(2)], start=(c == 0),
                                        stop=(c == CH - 1))
                last.then_inc(s_up, 1)

            convolve(0, 0)
            convolve(0, 1)
            project(0)
            dt_project(0, 0)
            dt_project(0, 1)
            convolve(1, 0)
            spread(0)
            convolve(1, 1)
            spread(1)
            for k in range(PAIRS * DS + 1):
                if k + 2 < PAIRS * DS:
                    spread(k + 2)
                if k == PAIRS * DS:
                    up(0, 0)
                if k:
                    for c in range(CH):
                        sum_n((k - 1) * CH + c)
                q, n = divmod(k, DS)
                if q == 0:
                    if n == 4:
                        project(1)
                    if n in (6, 7):
                        dt_project(1, n - 6)
                if q == 1:
                    if n in (2, 3):
                        transpose_y(0, n - 2)
                    if n == 7:
                        transpose_xf(0, 0)
                        transpose_xf(0, 1)
                    if n == 10:
                        logits(0)
                    if n == 14:
                        transpose_gates(0)

            def down(q, j):
                if q == 0 and j == 0:
                    pe.wait_ge(s_cbc, PAIRS * DS)
                    pe.wait_ge(s_x2, TP // 2)
                if q == 0:
                    pe.wait_ge(e_dn, min(j // 2 + 1, HC // 2))
                chunks = [j] if j < NE else list(range(NE, HC))
                pe.wait_ge(s_hid, q * HC + chunks[-1] + 1)
                if j == NE:
                    pe.wait_ge(l_b2, 32)
                    pe.wait_ge(s_gTe, q + 1)
                for g in range(2):
                    m = (q * (NE + 1) + j) * 2 + g
                    if m >= 3:
                        pe.wait_ge(s_acc, 2 * (m - 2))
                    for h in range(2):
                        t = 2 * g + h
                        po = p_o[m % 3][:, h * D:(h + 1) * D]
                        if j == NE:
                            nc.tensor.matmul(po, gatesT[:, (q * TP + t) * P:(q * TP + t + 1) * P], b2a[:], start=True, stop=False)
                        for jj in chunks:
                            slot = (q * HC + jj) % NHID
                            last = split_matmul(po, [part[:, slot, t * P:(t + 1) * P] for part in (hid_high, hid_low)],
                                                [w_dns[:, r, jj, :] for r in range(2)], start=(j < NE),
                                                stop=(jj == chunks[-1]))
                    last.then_inc(s_dn, 1)

            def experts_of(q):
                if q:
                    up(q, 0)
                up(q, 1)
                for j in range(NE):
                    up(q, j + 2)
                    down(q, j)
                    if q == 0:
                        if j in (0, 1):
                            transpose_y(1, j)
                        if j in (3, 4):
                            transpose_xf(1, j - 3)
                        if j == 6:
                            logits(1)
                    if q == 1 and j == 1:
                        transpose_gates(1)
                down(q, NE)

            experts_of(0)
            experts_of(1)


_INS = ['x', 'ctx_1024', 'L0_xattn_in_proj_w', 'L0_xattn_conv_w', 'L0_xattn_conv_b', 'L0_xattn_x_proj_w',
        'L0_xattn_dt_proj_w', 'L0_xattn_dt_proj_b', 'L0_xattn_A_log', 'L0_xattn_D', 'L0_ffn_gate_w', 'L0_ffn_w1',
        'L0_ffn_b1', 'L0_ffn_w2', 'L0_ffn_b2', 'L0_ffn_shared_w1', 'L0_ffn_shared_b1', 'L0_ffn_shared_w2',
        'L0_ffn_shared_b2']
_OUTS = [((4, 256, 256), 'float32')]


def kernel(**inputs):
    import numpy as _np
    import concourse.bacc as _bacc
    from concourse import mybir as _mybir
    from concourse.bass_utils import run_bass_kernel_spmd as _run

    nc = _bacc.Bacc("TRN2", target_bir_lowering=False, num_devices=1)
    arrays, args = {}, []
    for name in _INS:
        a = _np.ascontiguousarray(inputs[name])
        arrays[f"in_{name}_dram"] = a
        args.append(nc.dram_tensor(f"in_{name}_dram", a.shape, _mybir.dt.from_np(a.dtype), kind="ExternalInput").ap())
    for i, (shape, dtype) in enumerate(_OUTS):
        dt = _mybir.dt.from_np(_np.dtype(dtype))
        args.append(nc.dram_tensor(f"out_{i}_dram", shape, dt, kind="ExternalOutput").ap())
    mamba_xattn_moe_ffn(nc, *args)
    r = _run(nc, [arrays], core_ids=[0])
    got = tuple(r.results[0][f"out_{i}_dram"] for i in range(len(_OUTS)))
    return got[0]
```

```python
import math
from contextlib import ExitStack

import concourse.bass as bass
from concourse import mybir

F32 = mybir.dt.float32
F32R = mybir.dt.float32r
BF16 = mybir.dt.bfloat16
U32 = mybir.dt.uint32
ALU = mybir.AluOpType
ACT = mybir.ActivationFunctionType

P = 128
LN_EPS = 1e-5


def mamba_xattn_moe_ffn(
    nc: bass.Bass,
    x_in: bass.AP,
    ctx_in: bass.AP,
    in_proj_w: bass.AP,
    conv_w: bass.AP,
    conv_b: bass.AP,
    x_proj_w: bass.AP,
    dt_proj_w: bass.AP,
    dt_proj_b: bass.AP,
    A_log: bass.AP,
    D_skip: bass.AP,
    gate_w: bass.AP,
    w1: bass.AP,
    b1: bass.AP,
    w2: bass.AP,
    b2: bass.AP,
    shared_w1: bass.AP,
    shared_b1: bass.AP,
    shared_w2: bass.AP,
    shared_b2: bass.AP,
    out: bass.AP,
):
    B, L, DI = x_in.shape
    DM = ctx_in.shape[2]
    DC = conv_w.shape[1]
    DR = dt_proj_w.shape[1]
    DS = A_log.shape[1]
    NE, D, H = w1.shape
    CH = DI // P
    LT = L // P
    T = B * LT
    PAIRS = B // 2
    BP = B // PAIRS
    W = BP * L
    TP = T // PAIRS
    UNITS = DS * CH
    SUMS = (DS, DS - 2)
    SH = shared_w1.shape[1]
    HC = NE + SH // P
    PAD = DC - 1
    LP = L + PAD + 1
    assert DM == P and D == DI and H == P and W == 512 and CH == 2 and LT == 2
    BC = 2 * DS
    assert BC == 32
    XR = 3 * BC + DR

    with ExitStack() as ctx:

        def sb(name, shape, dt=F32):
            return ctx.enter_context(nc.sbuf_tensor(name, shape, dt))

        def sem(name):
            return ctx.enter_context(nc.semaphore(name))

        NA, NC, ND, NH, NP = 4, 3, 3, 3, 5
        NHID = 3

        x = sb("x", [P, T, D])
        ctx_nat = sb("ctx_nat", [P, T, DM])
        ctxT = sb("ctxT", [P, 2, B, LP], F32R)
        w_in = sb("w_in", [P, CH, DM])
        cw = sb("cw", [P, CH, DC])
        rows = sb("rows", [3 * CH + HC, P])
        cols = sb("cols", [P, 3 * CH + HC])
        cb = cols[:, 0:CH]
        dtb = cols[:, CH:2 * CH]
        dsk = cols[:, 2 * CH:3 * CH]
        b1T = cols[:, 3 * CH:3 * CH + HC]
        alog = sb("alog", [P, CH, DS])
        aneg = sb("aneg", [P, CH, DS])
        w_taps = sb("w_taps", [P, CH, DC, DM])
        w_tapsT = sb("w_tapsT", [P, 2, CH, DC, P], F32R)
        xp_nat = sb("xp_nat", [DR + BC, DI])
        xpT = sb("xpT", [P, CH, XR])
        dt_nat = sb("dt_nat", [P, CH, P])
        dtT = sb("dtT", [P, CH, P])
        skip = dt_nat
        ident = sb("ident", [P, P])
        minus_ident = sb("minus_ident", [P, P], F32R)
        selector = sb("selector", [3 * BC, BC], BF16)
        u = sb("u", [P, PAIRS, CH, W])
        sz = sb("sz", [P, PAIRS, CH, W])
        minus_half = sb("minus_half", [P, T])
        zstat = sb("zstat", [P, T, 6])
        zmv = sb("zmv", [P, T, 2])
        zrstd = sb("zrstd", [P, T])
        znmr = sb("znmr", [P, T])
        xdt = sb("xdt", [P, W])
        bc3 = sb("bc3", [3 * BC, PAIRS, W], BF16)
        bc_rest = sb("bc_rest", [2 * BC, W])
        vpos = sb("vpos", [P, CH, W])
        sp = sb("sp", [P, CH, W])
        delta = sb("delta", [P, PAIRS, CH, W])
        du = sb("du", [P, PAIRS, CH, W])
        decay_rest = sb("decay_rest", [P, NA - 1, CH, W])
        decay = [sz[:, 1]] + [decay_rest[:, i] for i in range(NA - 1)]
        c_bc = sb("c_bc", [P, NC, W])
        dbu = sb("dbu", [P, ND, CH, W])
        hst = sb("hst", [P, NH, CH, W])
        yt = w_taps[:].rearrange("p c k d -> p c (k d)")
        nstat = sb("nstat", [P, T, 6])
        nmv = sb("nmv", [P, T, 2])
        nrstd = sb("nrstd", [P, T])
        nnmr = sb("nnmr", [P, TP])
        e_base = sb("e_base", [P, TP])
        xf = ctx_nat[:].rearrange("p (t r) d -> p t (r d)", r=2)
        xfT = sb("xfT", [P, 2, CH, T * P], F32R)
        gw = sb("gw", [P, CH, NE])
        gws = sb("gws", [P, 2, CH, NE], F32R)
        lgT = bc_rest[0:NE, :]
        lg = sb("lg", [P, T, NE])
        mx = sb("mx", [P, T, 8])
        mi = sb("mi", [P, T, 8], U32)
        mif = sb("mif", [P, T, 2])
        gd = sb("gd", [P, T])
        ge = sb("ge", [P, T])
        gs = sb("gs", [P, T])
        g12 = sb("g12", [P, T, 2])
        experts = sb("experts", [P, NE])
        hot = sb("hot", [P, T, 2, NE])
        gates = sb("gates", [P, T, NE + 1])
        b2a = w_in[:].rearrange("p c d -> p (c d)")[0:NE + 1, :]
        b2s = sb("b2s", [NE + 1, 2, D], F32R)
        w_up = sb("w_up", [P, CH, HC, H])
        hc = w_up[:].rearrange("p c j h -> p (c j h)")[:, 0:NP * W].rearrange("p (s w) -> p s w", w=W)
        w_dn = sb("w_dn", [P, HC, D])
        w_ups = sb("w_ups", [P, 2, CH, HC, H], F32R)
        w_dns = sb("w_dns", [P, 2, HC, D], F32R)
        hid32 = sp
        hid_high = ctxT[:].rearrange("p r b l -> p (r b l)")[:, 0:NHID * W].rearrange("p (s w) -> p s w", w=W)
        hid_low = w_tapsT[:].rearrange("p r c k e -> p (r c) (k e)")[:, 0:NHID]
        gatesT = [ctxT[:].rearrange("p r b l -> p (r b l)")[0:NE + 1, NHID * W:(NHID + 1) * W],
                  w_tapsT[:].rearrange("p r c k e -> p (r c) (k e)")[0:NE + 1, NHID]]

        bank = [ctx.enter_context(nc.psum_tensor(f"bank{i}", [P, 512], F32)) for i in range(8)]
        p_b = [bank[0], bank[1]]
        p_c = [bank[2], bank[3]]
        p_sum = [[bank[5], bank[6]], [bank[4], bank[7]]]
        p_m = bank[7]
        p_up = [bank[5], bank[0], bank[1]]
        p_o = [bank[2], bank[3], bank[6]]

        l_ctx = [sem(f"l_ctx{q}") for q in range(PAIRS)]
        l_win = sem("l_win")
        l_xp = sem("l_xp")
        l_dt = sem("l_dt")
        l_vec = sem("l_vec")
        l_alog = sem("l_alog")
        l_x = [sem(f"l_x{q}") for q in range(PAIRS)]
        l_gw = sem("l_gw")
        l_b2 = sem("l_b2")
        h_b2 = sem("h_b2")
        e_b2 = sem("e_b2")
        h_gT = sem("h_gT")
        l_up = sem("l_up")
        l_dn = sem("l_dn")
        k_ident = sem("k_ident")
        k_sel = sem("k_sel")
        k_pool = sem("k_pool")
        k_warm = sem("k_warm")
        k_const = sem("k_const")
        k_zero = sem("k_zero")
        s_taps = sem("s_taps")
        t_taps = sem("t_taps")
        e_taps = sem("e_taps")
        t_ctx = sem("t_ctx")
        h_ctx = sem("h_ctx")
        h_taps = sem("h_taps")
        h_gw = sem("h_gw")
        e_gw = sem("e_gw")
        h_up = sem("h_up")
        h_dn = sem("h_dn")
        e_up = sem("e_up")
        e_dn = sem("e_dn")
        h_xfT = sem("h_xfT")
        s_hid32 = sem("s_hid32")
        e_ctx = sem("e_ctx")
        t_xp = sem("t_xp")
        e_xp = sem("e_xp")
        t_dt = sem("t_dt")
        e_dt = sem("e_dt")
        e_cols = sem("e_cols")
        s_aneg = sem("s_aneg")
        s_xc = sem("s_xc")
        s_u = sem("s_u")
        s_zst = sem("s_zst")
        s_zmv = sem("s_zmv")
        s_zr = sem("s_zr")
        s_z = sem("s_z")
        s_sz = sem("s_sz")
        s_xd = sem("s_xd")
        s_xdt = sem("s_xdt")
        s_hi = sem("s_hi")
        s_rest = sem("s_rest")
        s_mid = sem("s_mid")
        s_bc3 = sem("s_bc3")
        s_v = sem("s_v")
        s_abs = sem("s_abs")
        s_vpos = sem("s_vpos")
        s_ex = sem("s_ex")
        s_ln = sem("s_ln")
        s_delta = sem("s_delta")
        s_du = sem("s_du")
        s_B = sem("s_B")
        s_C = sem("s_C")
        s_cbc = sem("s_cbc")
        s_decay = sem("s_decay")
        s_dbu = sem("s_dbu")
        s_h = sem("s_h")
        s_first = sem("s_first")
        s_drive1 = sem("s_drive1")
        s_hc = sem("s_hc")
        s_y = sem("s_y")
        s_yf = sem("s_yf")
        s_tail = sem("s_tail")
        s_yT = sem("s_yT")
        s_x2 = sem("s_x2")
        s_nst = sem("s_nst")
        s_nmv = sem("s_nmv")
        s_nr = sem("s_nr")
        s_xf = sem("s_xf")
        s_xfT = sem("s_xfT")
        s_xfl = sem("s_xfl")
        s_xfTe = sem("s_xfTe")
        s_lg = sem("s_lg")
        s_lgT = sem("s_lgT")
        s_lgTe = sem("s_lgTe")
        s_lge = sem("s_lge")
        s_mx = sem("s_mx")
        s_mi = sem("s_mi")
        s_gd = sem("s_gd")
        s_ge = sem("s_ge")
        s_g = sem("s_g")
        s_gates = sem("s_gates")
        s_gT = sem("s_gT")
        s_gTe = sem("s_gTe")
        k_skip = sem("k_skip")
        s_nmr = sem("s_nmr")
        s_up = sem("s_up")
        s_hid = sem("s_hid")
        s_dn = sem("s_dn")
        s_acc = sem("s_acc")
        s_out = sem("s_out")

        x_tok = x_in.rearrange("b (t p) d -> p (b t) d", p=P)
        out_tok = out.rearrange("b (t p) d -> p (b t) d", p=P)
        ctx_tok = ctx_in.rearrange("b (t p) d -> p (b t) d", p=P)

        def as_rows(v):
            return v.rearrange("(c p) -> c p", p=P)

        def chans(v):
            return v.rearrange("(c p) k -> p c k", p=P)

        def batches(ap):
            return ap.rearrange("p (b l) -> p b l", b=BP)

        def conv_out(q, c):
            return p_sum[0][c] if q == 0 else (bank[4], p_m)[c]

        def ctx_out(q):
            return (p_b[0], p_c[1])[q]

        def dt_out(q, c):
            return p_b[c] if q == 0 else (bank[4], p_m)[c]

        def misc(q, g):
            return ((bank[5], bank[6]), (bank[4], bank[7]))[q][g]

        def groups_with(m):
            q, j = divmod(m, HC)
            return q * (NE + 1) + min(j, NE) + 1

        w_blocks = [(w_up[:, c, j:j + 5], w_ups[:, 0, c, j:j + 5], w_ups[:, 1, c, j:j + 5]) for j in (0, 5) for c in range(CH)]
        w_blocks += [(w_dn[:, j:j + 2], w_dns[:, 0, j:j + 2], w_dns[:, 1, j:j + 2]) for j in range(0, HC, 2)]

        UPS = 2 * CH

        def weights_low(engine, queue, k):
            raw, high, low = w_blocks[k]
            queue.wait_ge(h_up if k < UPS else h_dn, k + 1 if k < UPS else k + 1 - UPS)
            engine.tensor_tensor(low, raw, high.bitcast(F32), ALU.subtract).then_inc(e_up if k < UPS else e_dn, 1)

        last_n = hst[:, (PAIRS * DS - 1) % NH]
        assert (PAIRS * DS - 2) * CH % NP + CH <= NP

        def drive_factor(engine, queue, q, c):
            queue.wait_ge(s_delta, q * CH + c + 1)
            engine.tensor_tensor(du[:, q, c, :], delta[:, q, c, :], u[:, q, c, :], ALU.mult).then_inc(s_du, 1)

        block = ctx.enter_context(nc.Block())

        @block.sync
        def _(sp_):
            def load(dst, src, done):
                sp_.dma_start(dst, src).then_inc(done, 16)

            def load_ctx(q):
                load(ctx_nat[:, q * TP:(q + 1) * TP, :], ctx_tok[:, q * TP:(q + 1) * TP, :], l_ctx[q])

            load_ctx(0)
            load(xp_nat[:], x_proj_w, l_xp)
            for r, v in enumerate((conv_b, dt_proj_b, D_skip, shared_b1)):
                at = r * CH if r < 3 else 3 * CH + NE
                load(rows[at:at + CH, :], as_rows(v), l_vec)
            load(rows[3 * CH:3 * CH + NE, :], b1, l_vec)
            sp_.wait_ge(k_zero, 1)
            load(dt_nat[:, :, 3 * BC:XR], chans(dt_proj_w), l_dt)
            load(x[:, 0:TP], x_tok[:, 0:TP], l_x[0])
            load_ctx(1)
            load(x[:, TP:T], x_tok[:, TP:T], l_x[1])
            load(alog[:], chans(A_log), l_alog)
            load(gw[:], chans(gate_w), l_gw)
            for c in range(CH):
                load(w_up[:, c, 0:NE, :], w1[:, c * P:(c + 1) * P, :].rearrange("e p h -> p e h"), l_up)
                load(w_up[:, c, NE:HC, :], shared_w1[c * P:(c + 1) * P, :].rearrange("p (j h) -> p j h", h=H), l_up)
            load(w_dn[:, 0:NE, :], w2.rearrange("e p d -> p e d"), l_dn)
            load(w_dn[:, NE:HC, :], shared_w2.rearrange("(j p) d -> p j d", p=P), l_dn)
            sp_.wait_ge(s_taps, CH * DC)
            load(b2a[0:NE, :], b2, l_b2)
            load(b2a[NE:NE + 1, :], shared_b2.rearrange("(a d) -> a d", a=1), l_b2)
            for q in range(PAIRS):
                for t in range(TP):
                    sp_.wait_ge(s_acc, q * TP * (NE + 1) + TP * NE + t + 1)
                    sp_.dma_start(out_tok[:, q * TP + t, :], x[:, q * TP + t, :]).then_inc(s_out, 16)
            sp_.wait_ge(s_out, 16 * T)

        @block.gpsimd
        def _(pool):
            nc.gpsimd.memset(ident[:], 0.0).then_inc(k_pool, 1)
            pool.wait_ge(k_pool, 1)
            nc.gpsimd.affine_select(out=ident[:], in_=ident[:], compare_op=ALU.not_equal, fill=1.0, base=0,
                                    pattern=[[-1, P]], channel_multiplier=1).then_inc(k_ident, 1)
            nc.gpsimd.memset(ctxT[:, :, :, 0:PAD].bitcast(F32), 0.0).then_inc(k_const, 1)
            nc.gpsimd.memset(selector[:], 0.0).then_inc(k_pool, 1)
            pool.wait_ge(k_pool, 2)
            for r in range(3):
                nc.gpsimd.affine_select(out=selector[:], in_=selector[:], compare_op=ALU.not_equal, fill=1.0,
                                        base=-BC * r, pattern=[[-1, BC]], channel_multiplier=1).then_inc(k_sel, 1)
                pool.wait_ge(k_sel, r + 1)
            nc.gpsimd.memset(minus_half[:], -0.5).then_inc(k_const, 1)
            nc.gpsimd.iota(experts[:], [[1, NE]], base=0, channel_multiplier=0,
                           allow_small_or_imprecise_dtypes=True).then_inc(k_const, 1)
            nc.gpsimd.memset(gates[:, :, NE:NE + 1], 1.0).then_inc(k_const, 1)
            for slot in decay:
                nc.gpsimd.memset(slot.rearrange("p c (b l) -> p (c b) l", b=BP)[:, :, 0:1], 0.0).then_inc(k_const, 1)
            nc.gpsimd.memset(e_base[:], math.e).then_inc(k_const, 1)
            pool.wait_ge(k_const, 2)

            def rstd(o, var, steps, done):
                nc.gpsimd.tensor_scalar(o, var, LN_EPS, None, ALU.add).then_inc(k_pool, 1)
                pool.wait_ge(k_pool, steps)
                nc.gpsimd.tensor_tensor(o, o, minus_half[:, 0:var.shape[1]], ALU.pow).then_inc(done, 1)

            def z_rstd(q):
                pool.wait_ge(s_zmv, (q + 1) * TP)
                rstd(zrstd[:, q * TP:(q + 1) * TP], zmv[:, q * TP:(q + 1) * TP, 1], 3 + q, s_zr)

            z_rstd(0)
            pool.wait_ge(s_aneg, 1)
            nc.gpsimd.tensor_scalar(aneg[:], aneg[:], -1.0, None, ALU.mult).then_inc(s_aneg, 1)
            for k in range(UPS):
                weights_low(nc.gpsimd, pool, k)
            pool.wait_ge(e_up, UPS)

            def gate_exp(q):
                pool.wait_ge(s_gd, q + 1)
                pool.wait_ge(k_const, 5 + NA)
                a, b = q * TP, (q + 1) * TP
                nc.gpsimd.tensor_tensor(ge[:, a:b], e_base[:], gd[:, a:b], ALU.pow).then_inc(s_ge, 1)

            def token_rstd(q):
                a, b = q * TP, (q + 1) * TP
                pool.wait_ge(s_nmv, b)
                rstd(nrstd[:, a:b], nmv[:, a:b, 1], 3 + PAIRS + q, s_nr)

            for q in range(PAIRS):
                for n in range(DS):
                    if q == 0 and n == 8:
                        z_rstd(1)
                    if q == 1 and n == 5:
                        token_rstd(0)
                    k = q * DS + n
                    if k == PAIRS * DS - 1:
                        break
                    for c in range(CH):
                        i = k * CH + c
                        if i == 0:
                            pool.wait_ge(s_first, 1)
                        else:
                            pool.wait_ge(s_h, k + 1)
                        pool.wait_ge(s_cbc, k + 1)
                        if i >= NP:
                            pool.wait_ge(s_y, i - NP + 1)
                        nc.gpsimd.tensor_tensor(hc[:, i % NP, :], hst[:, k % NH, c, :], c_bc[:, k % NC, :], ALU.mult).then_inc(s_hc, 1)
            gate_exp(0)
            for m in range(PAIRS * HC):
                if m == 2:
                    pool.wait_ge(e_dn, 1)
                if m in (2, 4, 6, 8):
                    weights_low(nc.gpsimd, pool, UPS + m // 2)
                if m == 5:
                    token_rstd(1)
                if m == 6:
                    pool.wait_ge(h_b2, 1)
                    nc.gpsimd.tensor_tensor(b2s[:, 1], b2a[:], b2s[:, 0].bitcast(F32), ALU.subtract).then_inc(e_b2, 1)
                if m == HC + 1:
                    gate_exp(1)
                pool.wait_ge(s_hid32, m + 1)
                if m >= NHID:
                    pool.wait_ge(s_dn, 2 * groups_with(m - NHID))
                nc.gpsimd.tensor_tensor(hid_low[:, m % NHID, :], hid32[:, m % 2, :], hid_high[:, m % NHID, :].bitcast(F32),
                                        ALU.subtract).then_inc(s_hid, 1)

        @block.scalar
        def _(act):
            act.dma_start(w_in[:], chans(in_proj_w)).then_inc(l_win, 16)
            act.dma_start(cw[:], chans(conv_w)).then_inc(l_win, 16)
            nc.scalar.preload_act_table_set("silu_and_others")
            act.wait_ge(k_const, 1)

            act.wait_ge(t_ctx, 1)
            nc.scalar.copy(ctxT[:, 0, 0:BP, PAD:PAD + L], batches(ctx_out(0)[:])).then_inc(h_ctx, 1)
            for c in range(CH):
                act.wait_ge(t_taps, c + 1)
                nc.scalar.copy(w_tapsT[:, 0, c], p_sum[0][c][:].rearrange("p (k d) -> p k d", k=DC)).then_inc(h_taps, 1)

            def silu_u(q, c):
                act.wait_ge(s_xc, q * CH + c + 1)
                act.wait_ge(e_cols, 1)
                nc.scalar.activation(u[:, q, c, :], conv_out(q, c)[:], ACT.Silu, bias=cb[:, c:c + 1]).then_inc(s_u, 1)

            def silu_z(t):
                q = t // TP
                b, c = divmod(t - q * TP, LT)
                nc.scalar.activation(sz[:, q, c, b * L:(b + 1) * L], x[:, t, :], ACT.Silu, scale=zrstd[:, t:t + 1],
                                     bias=znmr[:, t:t + 1]).then_inc(s_sz, 1)

            def dt_rows(q):
                act.wait_ge(s_xd, q + 1)
                if q:
                    act.wait_ge(s_v, q * CH)
                nc.scalar.copy(xdt[3 * BC:XR, :], p_m[3 * BC:XR, :]).then_inc(s_xdt, 1)

            def softplus_abs(q, c):
                act.wait_ge(s_v, q * CH + c + 1)
                if q:
                    act.wait_ge(s_delta, c + 1)
                nc.scalar.activation(sp[:, c, :], dt_out(q, c)[:], ACT.Abs, bias=dtb[:, c:c + 1]).then_inc(s_abs, 1)

            def bc_high(q):
                nc.scalar.copy(bc3[:, q, :], p_m[0:3 * BC, :]).then_inc(s_hi, 1)

            def bc_middle(q):
                act.wait_ge(s_rest, q + 1)
                nc.scalar.copy(bc3[0:2 * BC, q, :], bc_rest[:]).then_inc(s_mid, 1)

            def positive(q, c):
                act.wait_ge(s_v, q * CH + c + 1)
                act.wait_ge(s_delta, c + 1)
                nc.scalar.activation(vpos[:, c, :], dt_out(q, c)[:], ACT.Relu, bias=dtb[:, c:c + 1]).then_inc(s_vpos, 1)

            def norm_scale(q):
                a = q * TP
                act.wait_ge(s_nmr, 1)
                for t in range(TP):
                    nc.scalar.activation(xf[:, t, :], x[:, a + t, :], ACT.Identity, scale=nrstd[:, a + t:a + t + 1],
                                         bias=nnmr[:, t:t + 1]).then_inc(s_xf, 1)

            def logits_out(q):
                act.wait_ge(s_lgT, q + 1)
                if q:
                    act.wait_ge(s_lg, q)
                nc.scalar.copy(lgT, misc(q, 1)[0:NE, :]).then_inc(s_lgTe, 1)

            def gatesT_out(q):
                act.wait_ge(s_gT, q + 1)
                if q:
                    act.wait_ge(s_dn, 2 * (NE + 1))
                nc.scalar.copy(gatesT[0], misc(1, q)[0:NE + 1, :]).then_inc(h_gT, 1)

            def softplus_exp(q, c):
                act.wait_ge(s_abs, q * CH + c + 1)
                nc.scalar.activation(sp[:, c, :], sp[:, c, :], ACT.Exp, scale=-1.0).then_inc(s_ex, 1)

            def softplus_log(q, c):
                act.wait_ge(s_ex, q * CH + c + 1)
                nc.scalar.activation(sp[:, c, :], sp[:, c, :], ACT.Ln, bias=1.0).then_inc(s_ln, 1)

            def weights_high(k):
                raw, high, low = w_blocks[k]
                act.wait_ge(l_dn, 32)
                nc.scalar.copy(high, raw).then_inc(h_dn, 1)

            def spread_C(k):
                act.wait_ge(s_C, k + 1)
                if k >= NC:
                    act.wait_ge(s_hc, (k - NC + 1) * CH)
                nc.scalar.copy(c_bc[:, k % NC, :], p_c[k % 2][:]).then_inc(s_cbc, 1)

            def xfT_low(q, c):
                act.wait_ge(s_xfl, q * CH + c + 1)
                nc.scalar.copy(xfT[:, 1, c, q * W:(q + 1) * W], misc(q, c)[:]).then_inc(s_xfTe, 1)

            def xfT_out(q, c):
                act.wait_ge(s_xfT, q * CH + c + 1)
                nc.scalar.copy(xfT[:, 0, c, q * W:(q + 1) * W], misc(q, c)[:]).then_inc(h_xfT, 1)

            silu_u(0, 0)
            silu_u(0, 1)
            nc.scalar.preload_act_table_set("natural_log_exp_and_others")
            dt_rows(0)
            bc_high(0)
            act.wait_ge(l_alog, 16)
            nc.scalar.activation(aneg[:], alog[:], ACT.Exp).then_inc(s_aneg, 1)
            softplus_abs(0, 0)
            bc_middle(0)
            softplus_exp(0, 0)
            softplus_log(0, 0)
            softplus_abs(0, 1)
            softplus_exp(0, 1)
            softplus_log(0, 1)
            act.wait_ge(s_aneg, 2)
            act.wait_ge(k_const, 4 + NA)
            for q in range(PAIRS):
                for n in range(DS):
                    for c in range(CH):
                        k = q * DS + n
                        if n == 0:
                            act.wait_ge(s_delta, q * CH + c + 1)
                        if k >= NA:
                            act.wait_ge(s_h, k - NA + 1)
                        nc.scalar.activation(batches(decay[k % NA][:, c, :])[:, :, 1:L], batches(delta[:, q, c, :])[:, :, 1:L],
                                             ACT.Exp, scale=aneg[:, c, n:n + 1]).then_inc(s_decay, 1)
                        if c == 0 and k != 1:
                            spread_C(max(k - 1, 0))
                    if q == 0 and n == 3:
                        nc.scalar.preload_act_table_set("silu_and_others")
                        silu_u(1, 0)
                        silu_u(1, 1)
                        nc.scalar.preload_act_table_set("natural_log_exp_and_others")
                    if q == 0 and n == 6:
                        dt_rows(1)
                    if q == 0 and n == 7:
                        bc_high(1)
                    if q == 0 and n in (9, 11):
                        positive(1, n // 2 - 4)
                        softplus_abs(1, n // 2 - 4)
                    if q == 0 and n in (10, 12):
                        softplus_exp(1, n // 2 - 5)
                        softplus_log(1, n // 2 - 5)
                    if q == 0 and n == 13:
                        bc_middle(1)
                    if q == 0 and n == 15:
                        nc.scalar.preload_act_table_set("silu_and_others")
                        act.wait_ge(s_z, 1)
                        for t in range(TP):
                            silu_z(t)
                        nc.scalar.preload_act_table_set("natural_log_exp_and_others")
                    if q == 1 and n in (1, 2, 3, 4, 5):
                        weights_high(UPS + n - 1)
                    if q == 1 and n == 9:
                        norm_scale(0)
                    if q == 1 and n == 12:
                        xfT_out(0, 0)
                        xfT_out(0, 1)
                    if q == 1 and n == 14:
                        xfT_low(0, 0)
                        xfT_low(0, 1)
            nc.scalar.preload_act_table_set("silu_and_others")
            spread_C(PAIRS * DS - 1)
            logits_out(0)
            act.wait_ge(s_h, PAIRS * DS - NA + 1)
            act.wait_ge(s_delta, PAIRS * CH)
            act.wait_ge(s_z, PAIRS)
            for t in range(TP, T):
                silu_z(t)
            nc.scalar.preload_act_table_set("gelu_and_others")
            for q in range(PAIRS):
                for j in range(HC):
                    m = q * HC + j
                    act.wait_ge(s_up, m + 1)
                    if m >= NHID:
                        act.wait_ge(s_dn, 2 * groups_with(m - NHID))
                    nc.scalar.activation(hid_high[:, m % NHID, :], p_up[m % 3][:], ACT.Gelu, bias=b1T[:, j:j + 1])
                    if m >= 2:
                        act.wait_ge(s_hid, m - 1)
                    nc.scalar.activation(hid32[:, m % 2, :], p_up[m % 3][:], ACT.Gelu, bias=b1T[:, j:j + 1]).then_inc(s_hid32, 1)
                    if q == 0 and j == 5:
                        act.wait_ge(l_b2, 32)
                        nc.scalar.copy(b2s[:, 0], b2a[:]).then_inc(h_b2, 1)
                    if q == 0 and j in (6, 7):
                        xfT_out(1, j - 6)
                    if q == 0 and j in (7, 8):
                        xfT_low(1, j - 7)
                    if (q, j) == (0, 9):
                        logits_out(1)
                    if j == 3:
                        gatesT_out(q)

        @block.vector
        def _(dve):
            nc.vector.memset(dt_nat[:], 0.0).then_inc(k_zero, 1)
            dve.wait_ge(l_win, 32)
            for c in range(CH):
                for k in range(DC):
                    nc.vector.tensor_scalar(w_taps[:, c, k, :], w_in[:, c, :], cw[:, c, k:k + 1], None, ALU.mult).then_inc(s_taps, 1)

            def ctx_low(q):
                dve.wait_ge(h_ctx, q + 1)
                ours = slice(q * BP, (q + 1) * BP)
                nc.vector.tensor_tensor(ctxT[:, 1, ours, PAD:PAD + L], batches(ctx_out(q)[:]),
                                        ctxT[:, 0, ours, PAD:PAD + L].bitcast(F32), ALU.subtract).then_inc(e_ctx, 1)

            ctx_low(0)
            for c in range(CH):
                dve.wait_ge(h_taps, c + 1)
                nc.vector.tensor_tensor(w_tapsT[:, 1, c], p_sum[0][c][:].rearrange("p (k d) -> p k d", k=DC),
                                        w_tapsT[:, 0, c].bitcast(F32), ALU.subtract).then_inc(e_taps, 1)
            dve.wait_ge(t_xp, 1)
            xpt = p_c[0][:, 0:CH * (DR + BC)].rearrange("p (c r) -> p c r", c=CH)
            for r in range(3):
                nc.vector.tensor_copy(xpT[:, :, r * BC:(r + 1) * BC], xpt[:, :, DR:DR + BC]).then_inc(e_xp, 1)
            nc.vector.tensor_copy(xpT[:, :, 3 * BC:XR], xpt[:, :, 0:DR]).then_inc(e_xp, 1)
            dve.wait_ge(t_dt, 1)
            nc.vector.tensor_copy(dtT[:], p_m[:, 0:CH * P].rearrange("p (c e) -> p c e", c=CH)).then_inc(e_dt, 1)
            nc.vector.tensor_copy(cols[:], p_m[:, CH * P:CH * P + 3 * CH + HC]).then_inc(e_cols, 1)

            def norm_z_stats(q, tiles):
                dve.wait_ge(l_x[q], 16)
                for t in tiles:
                    nc.vector.bn_stats(zstat[:, q * TP + t, :], x[:, q * TP + t, :]).then_inc(s_zst, 1)

            def norm_z(q):
                for t in range(q * TP, (q + 1) * TP):
                    dve.wait_ge(s_zst, t + 1)
                    nc.vector.bn_aggr(zmv[:, t, :], zstat[:, t, :]).then_inc(s_zmv, 1)

            def norm_z_offset(q):
                a, b = q * TP, (q + 1) * TP
                dve.wait_ge(s_zr, q + 1)
                nc.vector.scalar_tensor_tensor(znmr[:, a:b], zmv[:, a:b, 0], -1.0, zrstd[:, a:b], ALU.mult,
                                               ALU.mult).then_inc(s_z, 1)

            def bc_rests(q):
                dve.wait_ge(s_hi, q + 1)
                if q:
                    dve.wait_ge(s_bc3, q)
                nc.vector.tensor_tensor(bc_rest[:], p_m[0:2 * BC, :], bc3[0:2 * BC, q, :], ALU.subtract).then_inc(s_rest, 1)

            def bc_low(q):
                dve.wait_ge(s_mid, q + 1)
                third = bc3[BC:2 * BC, q, :]
                nc.vector.tensor_tensor(third, bc_rest[BC:2 * BC, :], third, ALU.subtract).then_inc(s_bc3, 1)

            def positive(q, c):
                dve.wait_ge(s_abs, q * CH + c + 1)
                nc.vector.tensor_scalar(vpos[:, c, :], dt_out(q, c)[:], dtb[:, c:c + 1], 0.0, ALU.add, ALU.max).then_inc(s_vpos, 1)

            def softplus_end(q, c):
                dve.wait_ge(s_ln, q * CH + c + 1)
                dve.wait_ge(s_vpos, q * CH + c + 1)
                nc.vector.tensor_tensor(delta[:, q, c, :], vpos[:, c, :], sp[:, c, :], ALU.add).then_inc(s_delta, 1)

            def drive(k):
                q, n = divmod(k, DS)
                if n == 0:
                    dve.wait_ge(s_du, (q + 1) * CH)
                dve.wait_ge(s_B, k + 1)
                if k >= ND:
                    dve.wait_ge(s_h, k - ND + 1)
                nc.vector.tensor_tensor(dbu[:, k % ND], du[:, q], p_b[n % 2][:].unsqueeze(1).to_broadcast([P, CH, W]),
                                        ALU.mult).then_inc(s_dbu, 1)

            def scan(k):
                dve.wait_ge(s_dbu, k + 1)
                dve.wait_ge(s_decay, (k + 1) * CH)
                if k >= NH:
                    dve.wait_ge(s_hc, (k - NH + 1) * CH)
                nc.vector.tensor_tensor_scan(*(slot.rearrange("p c w -> p (c w)") for slot in (
                    hst[:, k % NH], decay[k % NA], dbu[:, k % ND])), 0.0, ALU.mult, ALU.add).then_inc(s_h, 1)

            def drive_first(c):
                dve.wait_ge(s_du, c + 1)
                dve.wait_ge(s_B, 1)
                nc.vector.tensor_tensor(dbu[:, 0, c], du[:, 0, c], p_b[0][:], ALU.mult).then_inc((s_drive1, s_dbu)[c], 1)

            def scan_first(c):
                dve.wait_ge((s_drive1, s_dbu)[c], 1)
                dve.wait_ge(s_decay, c + 1)
                nc.vector.tensor_tensor_scan(hst[:, 0, c], decay[0][:, c], dbu[:, 0, c], 0.0, ALU.mult,
                                             ALU.add).then_inc((s_first, s_h)[c], 1)

            def finish_y(q):
                dve.wait_ge(s_y, sum(SUMS[:q + 1]) * CH)
                dve.wait_ge(s_sz, (q + 1) * TP)
                if q:
                    dve.wait_ge(s_yT, q * TP)
                for c in range(CH):
                    if q:
                        dve.wait_ge(s_tail, 2)
                        nc.vector.tensor_tensor(yt[:, c, :], p_sum[q][c][:], last_n[:, c, :], ALU.add).then_inc(s_tail, 1)
                        dve.wait_ge(s_tail, 3 + c)
                    nc.vector.tensor_tensor(yt[:, c, :], yt[:, c, :] if q else p_sum[q][c][:], sz[:, q, c, :],
                                            ALU.mult).then_inc(s_yf, 1)

            def last_product():
                n_last = PAIRS * DS - 1
                dve.wait_ge(s_cbc, n_last + 1)
                dve.wait_ge(s_h, n_last + 1)
                nc.vector.tensor_tensor(last_n, last_n, c_bc[:, n_last % NC, :].unsqueeze(1).to_broadcast([P, CH, W]),
                                        ALU.mult).then_inc(s_tail, 1)

            def last_sum():
                i = (PAIRS * DS - 2) * CH
                dve.wait_ge(s_hc, i + CH)
                dve.wait_ge(s_tail, 1)
                nc.vector.tensor_tensor(last_n, last_n, hc[:, i % NP:i % NP + CH, :], ALU.add).then_inc(s_tail, 1)

            def residual(q, g):
                t = q * TP + 2 * g
                dve.wait_ge(s_yT, t + 2)
                nc.vector.tensor_tensor(x[:, t:t + 2, :], x[:, t:t + 2, :], misc(q, g)[:].rearrange("p (t d) -> p t d", t=2),
                                        ALU.add).then_inc(s_x2, 1)

            def norm(q):
                a, b = q * TP, (q + 1) * TP
                dve.wait_ge(s_x2, b // 2)
                for t in range(a, b):
                    nc.vector.bn_stats(nstat[:, t, :], x[:, t, :]).then_inc(s_nst, 1)
                for t in range(a, b):
                    dve.wait_ge(s_nst, t + 1)
                    nc.vector.bn_aggr(nmv[:, t, :], nstat[:, t, :]).then_inc(s_nmv, 1)

            def norm_offset(q):
                a, b = q * TP, (q + 1) * TP
                dve.wait_ge(s_nr, q + 1)
                nc.vector.scalar_tensor_tensor(nnmr[:], nmv[:, a:b, 0], -1.0, nrstd[:, a:b], ALU.mult,
                                               ALU.mult).then_inc(s_nmr, 1)

            def gatesT_low(q):
                dve.wait_ge(h_gT, q + 1)
                nc.vector.tensor_tensor(gatesT[1], misc(1, q)[0:NE + 1, :], gatesT[0].bitcast(F32),
                                        ALU.subtract).then_inc(s_gTe, 1)

            def norm_scale(q):
                a, b = q * TP, (q + 1) * TP
                dve.wait_ge(s_nr, q + 1)
                for t in range(a, b):
                    nc.vector.tensor_scalar(xf[:, t - a, :], x[:, t, :], nmv[:, t, 0:1], nrstd[:, t:t + 1], ALU.subtract,
                                            ALU.mult).then_inc(s_xf, 1)

            def top2(q):
                a, b = q * TP, (q + 1) * TP
                dve.wait_ge(s_lg, q + 1)
                nc.vector.tensor_copy(lg[:, a:b, :], misc(q, 1)[:, 0:TP * NE].rearrange("p (t e) -> p t e", t=TP)).then_inc(s_lge, 1)
                dve.wait_ge(s_lge, q + 1)
                for t in range(a, b):
                    nc.vector.max(mx[:, t, :], lg[:, t, :]).then_inc(s_mx, 1)
                for t in range(a, b):
                    dve.wait_ge(s_mx, t + 1)
                    nc.vector.max_index(mi[:, t, :], mx[:, t, :], lg[:, t, :]).then_inc(s_mi, 1)
                nc.vector.tensor_tensor(gd[:, a:b], mx[:, a:b, 1], mx[:, a:b, 0], ALU.subtract).then_inc(s_gd, 1)
                dve.wait_ge(s_mi, b)
                nc.vector.tensor_copy(mif[:, a:b, :], mi[:, a:b, 0:2]).then_inc(s_g, 1)

            def gate(q):
                a, b = q * TP, (q + 1) * TP
                g = 8 * q
                dve.wait_ge(s_ge, q + 1)
                nc.vector.tensor_scalar(gs[:, a:b], ge[:, a:b], 1.0, None, ALU.add).then_inc(s_g, 1)
                dve.wait_ge(s_g, g + 2)
                nc.vector.reciprocal(g12[:, a:b, 0], gs[:, a:b]).then_inc(s_g, 1)
                dve.wait_ge(s_g, g + 3)
                nc.vector.tensor_tensor(g12[:, a:b, 1], ge[:, a:b], g12[:, a:b, 0], ALU.mult).then_inc(s_g, 1)
                dve.wait_ge(k_const, 4)
                for r in range(2):
                    nc.vector.tensor_tensor(hot[:, a:b, r, :], experts[:].unsqueeze(1).to_broadcast([P, TP, NE]),
                                            mif[:, a:b, r:r + 1].to_broadcast([P, TP, NE]), ALU.is_equal).then_inc(s_g, 1)
                    dve.wait_ge(s_g, g + 5 + r)
                for r in range(2):
                    nc.vector.tensor_tensor(hot[:, a:b, r, :], hot[:, a:b, r, :],
                                            g12[:, a:b, r:r + 1].to_broadcast([P, TP, NE]), ALU.mult).then_inc(s_g, 1)
                dve.wait_ge(s_g, g + 8)
                nc.vector.tensor_tensor(gates[:, a:b, 0:NE], hot[:, a:b, 0, :], hot[:, a:b, 1, :], ALU.add).then_inc(s_gates, 1)

            norm_z_stats(0, range(TP))
            norm_z(0)
            nc.vector.tensor_scalar(minus_ident[:], ident[:], -1.0, None, ALU.mult).then_inc(k_skip, 1)
            dve.wait_ge(e_cols, 1)
            for c in range(CH):
                nc.vector.tensor_scalar(skip[:, c], ident[:], dsk[:, c:c + 1], None, ALU.mult).then_inc(k_skip, 1)
            norm_z_offset(0)
            dve.wait_ge(l_gw, 16)
            nc.vector.tensor_copy(gws[:, 0], gw[:]).then_inc(h_gw, 1)
            dve.wait_ge(h_gw, 1)
            nc.vector.tensor_tensor(gws[:, 1], gw[:], gws[:, 0].bitcast(F32), ALU.subtract).then_inc(e_gw, 1)
            norm_z_stats(1, (0, 1))
            dve.wait_ge(t_ctx, 2)
            nc.vector.tensor_copy(ctxT[:, 0, BP:B, PAD:PAD + L], batches(ctx_out(1)[:])).then_inc(h_ctx, 1)
            ctx_low(1)
            dve.wait_ge(l_up, 64)
            for raw, high, low in w_blocks[0:UPS - 1]:
                nc.vector.tensor_copy(high, raw).then_inc(h_up, 1)
            bc_rests(0)
            nc.vector.tensor_copy(w_blocks[UPS - 1][1], w_blocks[UPS - 1][0]).then_inc(h_up, 1)
            norm_z_stats(1, (2,))
            positive(0, 0)
            bc_low(0)
            norm_z_stats(1, (3,))
            softplus_end(0, 0)
            drive_factor(nc.vector, dve, 0, 0)
            positive(0, 1)
            drive_first(0)
            scan_first(0)
            softplus_end(0, 1)
            drive_factor(nc.vector, dve, 0, 1)
            drive_first(1)
            scan_first(1)
            drive(1)
            for q in range(PAIRS):
                for n in range(DS):
                    k = q * DS + n
                    if 1 < k < PAIRS * DS - 1:
                        drive(k + 1)
                    if k:
                        scan(k)
                    if k == 1:
                        drive(k + 1)
                    if q == 0:
                        if n == 7:
                            bc_rests(1)
                            norm_z(1)
                        if n == 9:
                            norm_z_offset(1)
                        if n == 13:
                            bc_low(1)
                        if n in (10, 12):
                            softplus_end(1, n // 2 - 5)
                        if n in (11, 13):
                            drive_factor(nc.vector, dve, 1, n // 2 - 5)
                    if q == 1:
                        if n == 2:
                            finish_y(0)
                        if n == 3:
                            residual(0, 0)
                            residual(0, 1)
                        if n == 4:
                            norm(0)
                        if n == 6:
                            norm_offset(0)
            last_product()
            top2(0)
            weights_low(nc.vector, dve, UPS)
            last_sum()
            gate(0)
            finish_y(1)
            for q in range(PAIRS):
                dve.wait_ge(s_gates, q + 1)
                for j in range(NE + 1):
                    for t in range(TP):
                        m = (q * (NE + 1) + j) * 2 + t // 2
                        dve.wait_ge(s_dn, m + 1)
                        tile = q * TP + t
                        done = (q * (NE + 1) + j) * TP + t
                        if j:
                            dve.wait_ge(s_acc, done - TP + 1)
                        po = p_o[m % 3][:, (t % 2) * D:(t % 2 + 1) * D]
                        if j < NE:
                            nc.vector.scalar_tensor_tensor(x[:, tile, :], po, gates[:, tile, j:j + 1], x[:, tile, :],
                                                           ALU.mult, ALU.add).then_inc(s_acc, 1)
                        else:
                            nc.vector.tensor_tensor(x[:, tile, :], x[:, tile, :], po, ALU.add).then_inc(s_acc, 1)
                    if q == 0:
                        if j == 1:
                            residual(1, 0)
                            residual(1, 1)
                        if j == 2:
                            norm(1)
                            gatesT_low(0)
                        if j == 3:
                            norm_scale(1)
                        if j == 7:
                            top2(1)
                        if j == NE:
                            gate(1)
                    elif j == 3:
                        gatesT_low(1)

        @block.tensor
        def _(pe):
            def transpose(o, i):
                n = i.shape[0]
                return nc.tensor.transpose(o, i, ident[0:n, 0:n])

            def split_matmul(o, left, right, start=True, stop=True):
                nc.tensor.matmul(o, left[0], right[0], start=start, stop=False)
                nc.tensor.matmul(o, left[0], right[1], start=False, stop=False)
                return nc.tensor.matmul(o, left[1], right[0], start=False, stop=stop)

            def transpose_ctx(q):
                pe.wait_ge(l_ctx[q], 16)
                for t in range(TP):
                    last = transpose(ctx_out(q)[:, t * P:(t + 1) * P], ctx_nat[:, q * TP + t, :])
                last.then_inc(t_ctx, 1)

            pe.wait_ge(k_ident, 1)
            for _ in range(6):
                last = nc.tensor.matmul(p_m[:, 0:P], ident[:], ident[:], start=True, stop=True)
            last.then_inc(k_warm, 1)
            transpose_ctx(0)
            for c in range(CH):
                for k in range(DC):
                    pe.wait_ge(s_taps, c * DC + k + 1)
                    last = transpose(p_sum[0][c][:, k * P:(k + 1) * P], w_taps[:, c, k, :])
                last.then_inc(t_taps, 1)
            pe.wait_ge(l_xp, 16)
            for c in range(CH):
                last = transpose(p_c[0][:, c * (DR + BC):(c + 1) * (DR + BC)], xp_nat[:, c * P:(c + 1) * P])
            last.then_inc(t_xp, 1)
            pe.wait_ge(l_dt, 16)
            pe.wait_ge(l_vec, 80)
            pe.wait_ge(k_warm, 1)
            for c in range(CH):
                transpose(p_m[:, c * P:(c + 1) * P], dt_nat[:, c, :])
            transpose(p_m[:, CH * P:CH * P + 3 * CH + HC], rows[:]).then_inc(t_dt, 1)

            def convolve(q, c):
                pe.wait_ge(e_ctx, q + 1)
                pe.wait_ge(e_taps, c + 1)
                if q == 1 and c == 1:
                    pe.wait_ge(s_rest, 1)
                    pe.wait_ge(s_xdt, 1)
                ours = slice(q * BP, (q + 1) * BP)
                for k in range(DC):
                    last = split_matmul(conv_out(q, c)[:], [w_tapsT[:, r, c, k, :] for r in range(2)],
                                        [ctxT[:, r, ours, k:k + L] for r in range(2)], start=(k == 0), stop=(k == DC - 1))
                last.then_inc(s_xc, 1)

            def project(q):
                if q == 0:
                    pe.wait_ge(e_xp, 4)
                    pe.wait_ge(e_cols, 1)
                else:
                    pe.wait_ge(s_u, PAIRS * CH)
                for c in range(CH):
                    pe.wait_ge(s_u, q * CH + c + 1)
                    last = nc.tensor.matmul(p_m[0:XR, :], xpT[:, c, :], u[:, q, c, :], start=(c == 0), stop=(c == CH - 1))
                last.then_inc(s_xd, 1)

            def dt_project(q, c):
                pe.wait_ge(s_xdt, q + 1)
                if q == 1 and c == 1:
                    pe.wait_ge(s_rest, q + 1)
                nc.tensor.matmul(dt_out(q, c)[:], dtT[3 * BC:XR, c, :], xdt[3 * BC:XR, :], start=True,
                                 stop=True).then_inc(s_v, 1)

            def spread_b(k):
                q, n = divmod(k, DS)
                if n == 0:
                    pe.wait_ge(s_bc3, q + 1)
                    pe.wait_ge(k_sel, 3)
                if k < 2:
                    pe.wait_ge(s_vpos, k + 1)
                else:
                    pe.wait_ge(s_dbu, k - 1)
                nc.tensor.matmul(p_b[n % 2][:], selector[:, n:n + 1].to_broadcast([3 * BC, P]), bc3[:, q, :], start=True,
                                 stop=True).then_inc(s_B, 1)

            def spread_c(k):
                q, n = divmod(k, DS)
                if k >= 2:
                    pe.wait_ge(s_cbc, k - 1)
                elif k == 0:
                    pe.wait_ge(e_xp, 4)
                else:
                    pe.wait_ge(e_ctx, 2)
                nc.tensor.matmul(p_c[k % 2][:], selector[:, DS + n:DS + n + 1].to_broadcast([3 * BC, P]), bc3[:, q, :],
                                 start=True, stop=True).then_inc(s_C, 1)

            def start_sum(q):
                pe.wait_ge(k_skip, 1 + CH)
                for c in range(CH):
                    if q:
                        pe.wait_ge(s_abs, q * CH + c + 1)
                    nc.tensor.matmul(p_sum[q][c][:], skip[:, c], u[:, q, c, :], start=True, stop=False)

            def sum_n(i):
                q, n, c = i // UNITS, i % UNITS // CH, i % CH
                pe.wait_ge(s_hc, i + 1)
                nc.tensor.matmul(p_sum[q][c][:], ident[:], hc[:, i % NP, :], start=False,
                                 stop=(n == SUMS[q] - 1)).then_inc(s_y, 1)

            def transpose_y(q, g):
                pe.wait_ge(s_yf, (q + 1) * CH)
                for h in range(2):
                    for c in range(CH):
                        last = transpose(misc(q, g)[:, h * D + c * P:h * D + (c + 1) * P],
                                         yt[:, c, (2 * g + h) * P:(2 * g + h + 1) * P])
                    last.then_inc(s_yT, 1)

            def transpose_xf(q, c):
                pe.wait_ge(s_xf, (q + 1) * TP)
                for t in range(TP):
                    last = nc.tensor.matmul(misc(q, c)[:, t * P:(t + 1) * P], xf[:, t, c * P:(c + 1) * P], ident[:],
                                            is_transpose=True, start=(t == 0), stop=(t == TP - 1))
                last.then_inc(s_xfT, 1)

            def subtract_high(q, c):
                pe.wait_ge(h_xfT, q * CH + c + 1)
                nc.tensor.matmul(misc(q, c)[:], minus_ident[:], xfT[:, 0, c, q * W:(q + 1) * W], start=False,
                                 stop=True, skip_group_check=True).then_inc(s_xfl, 1)

            def logits(q):
                pe.wait_ge(s_xfTe, (q + 1) * CH)
                pe.wait_ge(e_gw, 1)
                for c in range(CH):
                    last = split_matmul(misc(q, 1)[0:NE, :], [gws[:, r, c, :] for r in range(2)],
                                        [xfT[:, r, c, q * W:(q + 1) * W] for r in range(2)], start=(c == 0),
                                        stop=(c == CH - 1))
                last.then_inc(s_lgT, 1)

            def transpose_logits(q):
                pe.wait_ge(s_lgTe, q + 1)
                for t in range(TP):
                    last = transpose(misc(q, 1)[:, t * NE:(t + 1) * NE], lgT[:, t * P:(t + 1) * P])
                last.then_inc(s_lg, 1)

            def transpose_gates(q):
                pe.wait_ge(s_gates, q + 1)
                pe.wait_ge(*((s_lge, PAIRS) if q else (s_x2, TP // 2 + 1)))
                for t in range(TP):
                    last = transpose(misc(1, q)[0:NE + 1, t * P:(t + 1) * P], gates[:, q * TP + t, :])
                last.then_inc(s_gT, 1)

            def up(q, j):
                m = q * HC + j
                if m == 0:
                    pe.wait_ge(e_up, UPS)
                if j == 0:
                    pe.wait_ge(s_xfTe, (q + 1) * CH)
                if m >= 3:
                    pe.wait_ge(s_hid32, m - 2)
                elif m == 0:
                    pe.wait_ge(s_xfTe, CH)
                else:
                    pe.wait_ge(s_dbu, PAIRS * DS - 2 + m)
                for c in range(CH):
                    last = split_matmul(p_up[m % 3][:], [w_ups[:, r, c, j, :] for r in range(2)],
                                        [xfT[:, r, c, q * W:(q + 1) * W] for r in range(2)], start=(c == 0),
                                        stop=(c == CH - 1))
                last.then_inc(s_up, 1)

            convolve(0, 0)
            convolve(0, 1)
            transpose_ctx(1)
            project(0)
            dt_project(0, 0)
            dt_project(0, 1)
            convolve(1, 0)
            spread_b(0)
            spread_c(0)
            convolve(1, 1)
            spread_b(1)
            start_sum(0)
            for k in range(PAIRS * DS + 1):
                if k + 2 < PAIRS * DS:
                    spread_b(k + 2)
                if k + 1 < PAIRS * DS:
                    spread_c(k + 1)
                if k == PAIRS * DS - 1:
                    up(0, 0)
                    transpose_logits(0)
                if 0 <= k - PAIRS * DS + 1 < 2:
                    up(0, k - PAIRS * DS + 2)
                if k == PAIRS * DS - 2:
                    logits(0)
                if 2 <= k < PAIRS * DS:
                    for c in range(CH):
                        sum_n((k - 2) * CH + c)
                q, n = divmod(k, DS)
                if q == 0:
                    if n == 4:
                        project(1)
                    if n == 12:
                        start_sum(1)
                    if n in (6, 8):
                        dt_project(1, n // 2 - 3)
                if q == 1:
                    if n == 2:
                        transpose_y(0, 0)
                        transpose_y(0, 1)
                    if n == 9:
                        transpose_xf(0, 0)
                        transpose_xf(0, 1)
                    if n == 11:
                        subtract_high(0, 0)
                        subtract_high(0, 1)

            def down(q, j):
                if q == 0 and j == 0:
                    pe.wait_ge(s_cbc, PAIRS * DS)
                if q == 0 and j == 1:
                    pe.wait_ge(s_lge, 1)
                if q == 0:
                    pe.wait_ge(e_dn, min(j // 2 + 1, HC // 2))
                chunks = [j] if j < NE else list(range(NE, HC))
                if j == NE:
                    pe.wait_ge(e_b2, 1)
                    pe.wait_ge(s_gTe, q + 1)
                banks = [(q * (NE + 1) + j) * 2 + g for g in range(2)]
                for jj in chunks:
                    pe.wait_ge(s_hid, q * HC + jj + 1)
                    for m, g in zip(banks, range(2)):
                        if m >= 3 and jj == chunks[0]:
                            pe.wait_ge(s_acc, 2 * (m - 2))
                        for h in range(2):
                            t = 2 * g + h
                            po = p_o[m % 3][:, h * D:(h + 1) * D]
                            if jj == NE:
                                split_matmul(po, [part[:, t * P:(t + 1) * P] for part in gatesT],
                                             [b2s[:, r, :] for r in range(2)], start=(h == 0), stop=False)
                            slot = (q * HC + jj) % NHID
                            last = split_matmul(po, [part[:, slot, t * P:(t + 1) * P] for part in (hid_high, hid_low)],
                                                [w_dns[:, r, jj, :] for r in range(2)], start=(j < NE),
                                                stop=(j < NE or (jj == chunks[-1] and h == 1)))
                        if jj == chunks[-1]:
                            last.then_inc(s_dn, 1)

            for q in range(PAIRS):
                for j in range(NE):
                    if q or j:
                        up(q, j + 2)
                    if (q, j) == (0, 5):
                        pe.wait_ge(s_gTe, 1)
                        transpose_xf(1, 0)
                        transpose_xf(1, 1)
                    down(q, j)
                    if q == 0:
                        if j == 1:
                            transpose_y(1, 0)
                            transpose_y(1, 1)
                        if j == 2:
                            transpose_gates(0)
                        if j in (5, 6):
                            subtract_high(1, j - 5)
                        if j == 7:
                            logits(1)
                            up(1, 0)
                            transpose_logits(1)
                            up(1, 1)
                    if q == 1 and j == 0:
                        transpose_gates(1)
                down(q, NE)


_INS = ['x', 'ctx_1024', 'L0_xattn_in_proj_w', 'L0_xattn_conv_w', 'L0_xattn_conv_b', 'L0_xattn_x_proj_w',
        'L0_xattn_dt_proj_w', 'L0_xattn_dt_proj_b', 'L0_xattn_A_log', 'L0_xattn_D', 'L0_ffn_gate_w', 'L0_ffn_w1',
        'L0_ffn_b1', 'L0_ffn_w2', 'L0_ffn_b2', 'L0_ffn_shared_w1', 'L0_ffn_shared_b1', 'L0_ffn_shared_w2',
        'L0_ffn_shared_b2']
_OUTS = [((4, 256, 256), 'float32')]


def kernel(**inputs):
    import numpy as _np
    import concourse.bacc as _bacc
    from concourse import mybir as _mybir
    from concourse.bass_utils import run_bass_kernel_spmd as _run

    nc = _bacc.Bacc("TRN2", target_bir_lowering=False, num_devices=1)
    arrays, args = {}, []
    for name in _INS:
        a = _np.ascontiguousarray(inputs[name])
        arrays[f"in_{name}_dram"] = a
        args.append(nc.dram_tensor(f"in_{name}_dram", a.shape, _mybir.dt.from_np(a.dtype), kind="ExternalInput").ap())
    for i, (shape, dtype) in enumerate(_OUTS):
        dt = _mybir.dt.from_np(_np.dtype(dtype))
        args.append(nc.dram_tensor(f"out_{i}_dram", shape, dt, kind="ExternalOutput").ap())
    mamba_xattn_moe_ffn(nc, *args)
    r = _run(nc, [arrays], core_ids=[0])
    got = tuple(r.results[0][f"out_{i}_dram"] for i in range(len(_OUTS)))
    return got[0]
```
